# Optimizing a Trainium2 kernel written in Bass

```python
import numpy as np
import jax
import jax.numpy as jnp

def _softmax(x, axis=-1):
    return jax.nn.softmax(x, axis=axis)

def _gelu(x):
    return jax.nn.gelu(x, approximate=True)

def _silu(x):
    return jax.nn.silu(x)

def _sigmoid(x):
    return jax.nn.sigmoid(x)

def _layernorm(x, axis=-1, eps=1e-05):
    m = jnp.mean(x, axis=axis, keepdims=True)
    v = jnp.var(x, axis=axis, keepdims=True)
    return (x - m) / jnp.sqrt(v + eps)

def _scatter_add(tgt, idx, src, axis=0):
    return tgt.at[idx].add(src)

def _segment_sum(src, seg, n):
    return jax.ops.segment_sum(src, seg, n)
kernel_name = 'mk_xattn_ffn_d1_seqx_r8_f5a9f1'

def setup_inputs(seed: int=0):
    np.random.seed(seed)
    _w = jnp.asarray

    def _rec_inputs():
        import jax
        import jax.numpy as jnp
        _rk = jax.random.key(seed)
        x = 0.0002417 + 0.9998 * jax.random.normal(jax.random.fold_in(_rk, 1), (16, 256, 128), jnp.float32)
        _lenS = 256 - jax.random.randint(jax.random.fold_in(_rk, 7), (16,), 0, max(1, 256 // 4) + 1, jnp.int32)
        _lenS2 = 64 - jax.random.randint(jax.random.fold_in(_rk, 8), (16,), 0, max(1, 64 // 4) + 1, jnp.int32)
        _ctx_1024P = jax.random.normal(jax.random.fold_in(_rk, 11), (16, 16, 128), jnp.float32)
        _ctx_1024c = jax.random.dirichlet(jax.random.fold_in(_rk, 511), 0.3 * jnp.ones((16,), jnp.float32), (16, 64))
        _ctx_1024t = jnp.einsum('bsk,bkd->bsd', _ctx_1024c, _ctx_1024P)
        _ctx_1024t = _ctx_1024t * jax.lax.rsqrt(jnp.mean(jnp.square(_ctx_1024t)) + 1e-12) * 0.953939
        ctx_1024 = 7.22013e-05 + 1.00017 * (_ctx_1024t + 0.3 * jax.random.normal(jax.random.fold_in(_rk, 611), (16, 64, 128), jnp.float32))
        return (x, ctx_1024)
    x, ctx_1024 = _rec_inputs()

    def _L0_xattn_setup():
        import jax, jax.numpy as jnp
        import numpy as np
        D_MODEL = 128
        B, S = (4, 256)
        key = jax.random.key(seed)
        ks = jax.random.split(key, 10)
        s = 1.0 / np.sqrt(D_MODEL)
        return {'k': jax.random.normal(ks[0], (B, S, D_MODEL), jnp.float32), 'v': jax.random.normal(ks[1], (B, S, D_MODEL), jnp.float32), 'q': jax.random.normal(ks[2], (B, S, D_MODEL), jnp.float32), 'Wk': jax.random.normal(ks[3], (D_MODEL, D_MODEL), jnp.float32) * s, 'Wv': jax.random.normal(ks[4], (D_MODEL, D_MODEL), jnp.float32) * s, 'bv': jnp.zeros((D_MODEL,), jnp.float32), 'Wq': jax.random.normal(ks[5], (D_MODEL, D_MODEL), jnp.float32) * s, 'bq': jnp.zeros((D_MODEL,), jnp.float32), 'Wo': jax.random.normal(ks[6], (D_MODEL, D_MODEL), jnp.float32) * s, 'bo': jnp.zeros((D_MODEL,), jnp.float32)}
    _L0_xattn_all = _L0_xattn_setup()
    _L0_xattn_in = {k: v for k, v in _L0_xattn_all.items() if k in ('Wk', 'Wv', 'bv', 'Wq', 'bq', 'Wo', 'bo')}
    del _L0_xattn_all

    def _L0_ffn_setup():
        import jax, jax.numpy as jnp
        import numpy as np
        E = 8
        K = 2
        D = 128
        F = 512
        EPS = 1e-05

        def _layernorm(h, g, b):
            mu = h.mean(axis=-1, keepdims=True)
            var = ((h - mu) ** 2).mean(axis=-1, keepdims=True)
            return (h - mu) * jax.lax.rsqrt(var + EPS) * g[:, None, :] + b[:, None, :]
        key = jax.random.key(seed)
        ks = jax.random.split(key, 8)
        B, S = (2, 256)
        x = jax.random.normal(ks[0], (B, S, D), dtype=jnp.float32)
        Wr = jax.random.normal(ks[1], (D, E), dtype=jnp.float32) / np.sqrt(D)
        br = jnp.zeros((E,), dtype=jnp.float32)
        W1 = jax.random.normal(ks[2], (E, D, F), dtype=jnp.float32) / np.sqrt(D)
        b1 = jnp.zeros((E, F), dtype=jnp.float32)
        g1 = jnp.ones((E, F), dtype=jnp.float32)
        be1 = jnp.zeros((E, F), dtype=jnp.float32)
        W2 = jax.random.normal(ks[3], (E, F, D), dtype=jnp.float32) / np.sqrt(F)
        b2 = jnp.zeros((E, D), dtype=jnp.float32)
        g2 = jnp.ones((E, D), dtype=jnp.float32)
        be2 = jnp.zeros((E, D), dtype=jnp.float32)
        return {'x': x, 'Wr': Wr, 'br': br, 'W1': W1, 'b1': b1, 'g1': g1, 'be1': be1, 'W2': W2, 'b2': b2, 'g2': g2, 'be2': be2}
    _L0_ffn_all = _L0_ffn_setup()
    _L0_ffn_in = {k: v for k, v in _L0_ffn_all.items() if k in ('Wr', 'br', 'W1', 'b1', 'g1', 'be1', 'W2', 'b2', 'g2', 'be2')}
    del _L0_ffn_all
    return {'x': x, 'ctx_1024': ctx_1024, 'L0_xattn_Wk': _L0_xattn_in['Wk'], 'L0_xattn_Wv': _L0_xattn_in['Wv'], 'L0_xattn_bv': _L0_xattn_in['bv'], 'L0_xattn_Wq': _L0_xattn_in['Wq'], 'L0_xattn_bq': _L0_xattn_in['bq'], 'L0_xattn_Wo': _L0_xattn_in['Wo'], 'L0_xattn_bo': _L0_xattn_in['bo'], 'L0_ffn_Wr': _L0_ffn_in['Wr'], 'L0_ffn_br': _L0_ffn_in['br'], 'L0_ffn_W1': _L0_ffn_in['W1'], 'L0_ffn_b1': _L0_ffn_in['b1'], 'L0_ffn_g1': _L0_ffn_in['g1'], 'L0_ffn_be1': _L0_ffn_in['be1'], 'L0_ffn_W2': _L0_ffn_in['W2'], 'L0_ffn_b2': _L0_ffn_in['b2'], 'L0_ffn_g2': _L0_ffn_in['g2'], 'L0_ffn_be2': _L0_ffn_in['be2']}

def reference(x, ctx_1024, L0_xattn_Wk, L0_xattn_Wv, L0_xattn_bv, L0_xattn_Wq, L0_xattn_bq, L0_xattn_Wo, L0_xattn_bo, L0_ffn_Wr, L0_ffn_br, L0_ffn_W1, L0_ffn_b1, L0_ffn_g1, L0_ffn_be1, L0_ffn_W2, L0_ffn_b2, L0_ffn_g2, L0_ffn_be2):
    import jax
    import jax.numpy as jnp

    def _L0_xattn_ref(k, v, q, Wk, Wv, bv, Wq, bq, Wo, bo):
        import jax, jax.numpy as jnp
        import numpy as np
        D_MODEL = 128
        B, S = (4, 256)
        kp = jnp.einsum('bsd,ed->bse', k, Wk)
        vp = jnp.einsum('bsd,ed->bse', v, Wv) + bv
        qp = jnp.einsum('bsd,ed->bse', q, Wq) + bq
        scale = 1.0 / jnp.sqrt(jnp.float32(kp.shape[-1]))
        scores = jnp.einsum('bqd,bkd->bqk', qp, kp) * scale
        probs = jax.nn.softmax(scores, axis=-1)
        ctx = jnp.einsum('bqk,bkd->bqd', probs, vp)
        return jnp.einsum('bqd,ed->bqe', ctx, Wo) + bo

    def _L0_ffn_ref(x, Wr, br, W1, b1, g1, be1, W2, b2, g2, be2):
        import jax, jax.numpy as jnp
        import numpy as np
        E = 8
        K = 2
        D = 128
        F = 512
        EPS = 1e-05

        def _layernorm(h, g, b):
            mu = h.mean(axis=-1, keepdims=True)
            var = ((h - mu) ** 2).mean(axis=-1, keepdims=True)
            return (h - mu) * jax.lax.rsqrt(var + EPS) * g[:, None, :] + b[:, None, :]
        B, S, _ = x.shape
        xt = x.reshape(-1, D)
        logits = xt @ Wr + br
        p = jax.nn.softmax(logits, axis=-1)
        probs, idx = jax.lax.top_k(p, K)
        probs = probs / probs.sum(axis=-1, keepdims=True)
        h = jnp.einsum('td,edf->etf', xt, W1) + b1[:, None, :]
        h = _layernorm(jax.nn.relu(h), g1, be1)
        y = jnp.einsum('etf,efd->etd', h, W2) + b2[:, None, :]
        y = _layernorm(jax.nn.relu(y), g2, be2)
        gate = (jax.nn.one_hot(idx, E, dtype=x.dtype) * probs[..., None]).sum(axis=1)
        out = jnp.einsum('te,etd->td', gate, y)
        return out.reshape(B, S, D)
    x = x + _L0_xattn_ref(ctx_1024, ctx_1024, _layernorm(x, axis=-1), L0_xattn_Wk, L0_xattn_Wv, L0_xattn_bv, L0_xattn_Wq, L0_xattn_bq, L0_xattn_Wo, L0_xattn_bo)
    x = x + _L0_ffn_ref(_layernorm(x, axis=-1), L0_ffn_Wr, L0_ffn_br, L0_ffn_W1, L0_ffn_b1, L0_ffn_g1, L0_ffn_be1, L0_ffn_W2, L0_ffn_b2, L0_ffn_g2, L0_ffn_be2)
    return x

_drawn_inputs = setup_inputs


def setup_inputs(seed=0):
    import zlib

    import numpy as np

    out = dict(_drawn_inputs(seed))
    spreads = {'L0_xattn_bv': (0.0, 0.1),
     'L0_xattn_bq': (0.0, 0.1),
     'L0_xattn_bo': (0.0, 0.1),
     'L0_ffn_br': (0.0, 0.1),
     'L0_ffn_b1': (0.0, 0.1),
     'L0_ffn_g1': (1.0, 0.2),
     'L0_ffn_be1': (0.0, 0.1),
     'L0_ffn_b2': (0.0, 0.1),
     'L0_ffn_g2': (1.0, 0.2),
     'L0_ffn_be2': (0.0, 0.1)}
    factors = {}
    for name, (base, spread) in spreads.items():
        noise = np.random.default_rng([zlib.crc32(name.encode()), seed]).standard_normal(out[name].shape)
        drawn = base * np.exp(spread * noise) if base else spread * noise
        out[name] = jnp.asarray(drawn.astype(out[name].dtype))
    for name, factor in factors.items():
        out[name] = (out[name] * factor).astype(out[name].dtype)
    return out
```

```python
import concourse.bass as bass
import numpy as np
from concourse import mybir
from contextlib import ExitStack

F32, F16, BF16, U32, I32 = (mybir.dt.float32, mybir.dt.float16, mybir.dt.bfloat16, mybir.dt.uint32,
                            mybir.dt.int32)
ALU = mybir.AluOpType
ACT = mybir.ActivationFunctionType
AX = mybir.AxisListType


class Signal:

    def __init__(self, handle):
        self.handle, self.count = handle, 0


class Program:

    def __init__(self):
        self.queues = {n: [] for n in ("sync", "gpsimd", "scalar", "tensor", "vector")}
        self.waited = {}

    def add(self, engine, issue, after=(), signal=None, inc=1):
        waits = []
        for event in after:
            if event is None:
                continue
            sig, value = event
            if self.waited.get((engine, sig), 0) < value:
                self.waited[engine, sig] = value
                waits.append((sig.handle, value))
        if signal is not None:
            signal.count += inc

        def run(eng):
            for handle, value in waits:
                eng.wait_ge(handle, value)
            ins = issue(eng)
            if signal is not None:
                ins.then_inc(signal.handle, inc)

        self.queues[engine].append(run)
        return None if signal is None else (signal, signal.count)


def build(nc, A, out):
    P = 128
    B, S, D = A["x"].shape
    KEYS = A["ctx_1024"].shape[1]
    TOKENS = B * S
    TILES = TOKENS // P
    E, _, F = A["L0_ffn_W1"].shape
    K = 2
    FC = F // P
    GT = 4
    GROUPS = TILES // GT
    EPS = 1e-5
    SCALE = float(D) ** -0.5
    CTX_TILES = B * KEYS // P
    REGION = TOKENS + P
    SLOT_TILES = K * TOKENS // P + E - 1
    TRASH = SLOT_TILES * P
    ROW = 2 * D + 2
    GUARD = 16.0
    assert GT * P == 2 * S and 2 * KEYS == P

    pr = Program()
    ctx = ExitStack()
    with ctx:
        def sb(name, shape, dt=F32):
            return ctx.enter_context(nc.sbuf_tensor(name, shape, dt))

        def signal(name):
            return Signal(ctx.enter_context(nc.semaphore(name)))

        bank = [ctx.enter_context(nc.psum_tensor(f"bank{i}", [P, 512], F32)) for i in range(8)]

        slots = nc.dram_tensor("slot_rows", (E * REGION + P, ROW), F16).ap()
        answers = nc.dram_tensor("answers", (TRASH + K * TOKENS, D), F32).ap()

        x_in = A["x"].rearrange("b s d -> (b s) d").rearrange("(i p) d -> p i d", p=P)
        out_v = out.rearrange("b s d -> (b s) d").rearrange("(i p) d -> p i d", p=P)
        ctx_in = A["ctx_1024"].rearrange("b s d -> (b s) d").rearrange("(i p) d -> p i d", p=P)
        ans_v = answers[TRASH:, :].rearrange("(i p) d -> p i d", p=P)

        ones = sb("ones", [P, P])
        ones16 = sb("ones16", [P, P], F16)
        ident = sb("ident", [P, P])
        ident16 = sb("ident16", [P, P], F16)
        mean_w = sb("mean_w", [P, P])
        below = sb("below", [P, P], BF16)
        onesb = sb("onesb", [P, P], BF16)
        iota_e = sb("iota_e", [P, GT, E])
        zero_rows = sb("zero_rows", [P, ROW], F16)
        trash_row = sb("trash_row", [P, SLOT_TILES])
        home_row = sb("home_row", [P, K, TILES], U32)
        tri = sb("tri", [1, E, E])
        slot_no = sb("slot_no", [1, SLOT_TILES])
        region0 = sb("region0", [P, E])

        x = sb("x_tok", [P, TILES, D])
        x2 = sb("x2", [P, TILES, D])
        cx = sb("cx", [P, CTX_TILES, D])
        cxT = sb("cxT", [P, CTX_TILES * P])
        w4 = sb("w4", [P, 4, D])
        woT = sb("woT", [P, D])
        wkq = sb("wkq", [P, D])
        wvo = sb("wvo", [P, D])
        bcol = sb("bcol", [P, 2])
        borow = sb("borow", [1, D])
        kb_col = sb("kb_col", [P, 1])
        vb_row = sb("vb_row", [1, D])
        kq = sb("kq", [P, CTX_TILES * P])
        kb_row = sb("kb_row", [1, CTX_TILES * P])
        vo = sb("vo", [P, CTX_TILES, D])
        wr = sb("wr", [P, E])
        brrow = sb("brrow", [1, E])

        w1f = sb("w1f", [P, E * F])
        w2f = sb("w2f", [P, E * FC, D])
        w1h = sb("w1h", [P, E * F], F16)
        w1l = sb("w1l", [P, E * F], F16)
        w2h = sb("w2h", [P, E * F], F16)
        w2l = sb("w2l", [P, E * F], F16)
        w2g = sb("w2g", [P, FC, D])
        w2c = sb("w2c", [P, FC, D])
        NB = E * F // P
        b1c = sb("b1c", [P, NB])
        b1h = sb("b1h", [P, NB], F16)
        b1l = sb("b1l", [P, NB], F16)
        b1t = sb("b1t", [P, E * F], F16)
        gb = sb("gb", [2 * NB, P])
        gbT = sb("gbT", [P, 2 * NB])
        g1c, be1c = gbT[:, 0:NB], gbT[:, NB:2 * NB]
        b2row = sb("b2row", [1, E * D])
        c2row = sb("c2row", [1, E * D])
        c2 = sb("c2", [P, E * D])
        g2 = sb("g2", [P, E * D])
        be2 = sb("be2", [P, E * D])
        mx = sb("mx", [P, 4])
        mx4 = sb("mx4", [4, 1])
        dg4 = sb("dg4", [4, 4])
        mb = sb("mb", [P, 4])
        mm2 = sb("mm2", [P, 2])
        pw2 = sb("pw2", [P, 2], U32)
        sc = sb("sc", [P, 2])
        scg = sb("scg", [P, 2])
        sc2 = sb("sc2", [P, 2])
        epsS = sb("epsS", [P, 2])

        st = sb("st", [P, 2, GT, 6])
        mv = sb("mv", [P, 2, GT, 2])
        ve = sb("ve", [P, 2, GT])
        lnv = sb("lnv", [P, 2, GT])
        y0 = sb("y0", [P, 2, GT])
        yy = sb("yy", [P, 2, GT])
        yv = sb("yv", [P, 2, GT])
        yt = sb("yt", [P, 2, GT])
        rstd = sb("rstd", [P, 2, GT])
        xn = sb("xn", [P, GT, D])
        xnT = sb("xnT", [P, GT * P])
        smax = sb("smax", [P, 2, 2])
        nmax = sb("nmax", [P, 2, 2])
        prob = sb("prob", [P, 2, 2, KEYS])
        psum_ = sb("psum_", [P, 2, 2])
        rsum = sb("rsum", [P, 2, 2])
        pT = sb("pT", [P, 2, P])
        xt = sb("xt", [P, GT, D])
        xtT = sb("xtT", [P, GT * P])
        lg = sb("lg", [P, GT, E])
        top = sb("top", [P, TILES, 8])
        topi = sb("topi", [P, GT, 8], U32)
        oh = sb("oh", [P, K, GT, E])
        mask = sb("mask", [P, GT, E], BF16)
        filled = sb("filled", [P, 2, E])
        rank = sb("rank", [P, GT, E])
        pick = sb("pick", [P, K, GT, E])
        posf = sb("posf", [P, K, GT])
        pos = sb("pos", [P, 2, K, GT], U32)
        pay = [sb(f"pay{n}", [P, K, GT, ROW], F16) for n in range(2)]
        gd = sb("gd", [P, TILES])
        ge_ = sb("ge_", [P, TILES])
        gs = sb("gs", [P, TILES])
        gate = sb("gate", [P, K, TILES])

        cnt = sb("cnt", [1, E])
        cnti = sb("cnti", [1, E], I32)
        cnt2 = sb("cnt2", [1, E], I32)
        nti = sb("nti", [1, E], I32)
        ntf = sb("ntf", [1, E])
        ntri = sb("ntri", [1, E, E])
        cum = sb("cum", [1, E])
        full = sb("full", [1, SLOT_TILES, E])
        fulln = sb("fulln", [1, SLOT_TILES, E])
        sx = sb("sx", [1, SLOT_TILES])
        sfirst = sb("sfirst", [1, SLOT_TILES])
        sa = sb("sa", [1, SLOT_TILES])
        sb_ = sb("sb_", [1, SLOT_TILES])
        smin = sb("smin", [1, SLOT_TILES])
        row_tab = sb("row_tab", [1, SLOT_TILES], U32)
        off_w = sb("off_w", [1, SLOT_TILES], U32)
        off_d = sb("off_d", [1, SLOT_TILES], U32)
        tailf = sb("tailf", [1, E])
        tail = sb("tail", [1, E], U32)

        NX = 4
        NZ = 3
        xs = [sb(f"xs{n}", [P, ROW], F16) for n in range(NX)]
        xsT = [sb(f"xsT{n}", [P, 2 * P], F16) for n in range(2)]
        r = [sb(f"r{n}", [P, F]) for n in range(2)]
        rTh = [sb(f"rTh{n}", [P, F], F16) for n in range(2)]
        rTl = [sb(f"rTl{n}", [P, F], F16) for n in range(2)]
        st1 = [sb(f"st1_{n}", [P, 6]) for n in range(4)]
        mv1 = [sb(f"mv1_{n}", [P, 2]) for n in range(4)]
        sd1 = [sb(f"sd1_{n}", [P, 1]) for n in range(4)]
        rs1 = [sb(f"rs1_{n}", [P, 1]) for n in range(4)]
        u = [sb(f"u{n}", [P, D]) for n in range(3)]
        ur = [sb(f"ur{n}", [P, D]) for n in range(3)]
        st2 = [sb(f"st2_{n}", [P, 6]) for n in range(4)]
        mv2 = [sb(f"mv2_{n}", [P, 2]) for n in range(4)]
        sd2 = [sb(f"sd2_{n}", [P, 1]) for n in range(4)]
        rs2 = [sb(f"rs2_{n}", [P, 1]) for n in range(4)]
        z0 = [sb(f"z0_{n}", [P, D]) for n in range(2)]
        z1 = [sb(f"z1_{n}", [P, D]) for n in range(2)]
        z = [sb(f"z{n}", [P, D]) for n in range(NZ)]
        ND = 9
        dest = [sb(f"dest{n}", [P, 1], U32) for n in range(ND)]
        GD = GT * D

        def part_c(at, n):
            return w1f[:, at * GD:(at + n) * GD].rearrange("p (k i d) -> p k i d", k=n, i=GT)

        ya = [part_c(n * K, K) for n in range(2)]
        acc = [part_c(2 * K + n, 1)[:, 0, :, :] for n in range(2)]
        res = [part_c(2 * K + 2 + n, 1)[:, 0, :, :] for n in range(2)]

        def load(name, dst, src, engine="sync"):
            return pr.add(engine, lambda e: e.dma_start(dst, src), signal=signal("ld_" + name), inc=16)

        ev_cx = load("ctx", cx[:, :, :], ctx_in)
        ev_w4 = {n: load(n, w4[:, q, :], A[f"L0_xattn_{n}"], "scalar")
                 for q, n in enumerate(("Wk", "Wq", "Wv", "Wo"))}
        WK, WQ, WV, WO = (w4[:, q, :] for q in range(4))
        ev_bq = load("bq", bcol[:, 0:1], A["L0_xattn_bq"].rearrange("(p o) -> p o", o=1), "scalar")
        ev_bv = load("bv", bcol[:, 1:2], A["L0_xattn_bv"].rearrange("(p o) -> p o", o=1), "scalar")
        ev_bo = load("bo", borow[:, :], A["L0_xattn_bo"].rearrange("(o n) -> o n", o=1), "scalar")
        ev_x = [load(f"x{g}", x[:, g * GT:(g + 1) * GT, :], x_in[:, g * GT:(g + 1) * GT, :])
                for g in range(GROUPS)]
        ev_wr = load("wr", wr[:, :], A["L0_ffn_Wr"], "scalar")
        ev_br = load("br", brrow[:, :], A["L0_ffn_br"].rearrange("(o n) -> o n", o=1), "scalar")
        H = E // 2
        ev_w1 = [load(f"w1_{h}", w1f[:, h * H * F:(h + 1) * H * F].rearrange("p (e f) -> p e f", e=H),
                      A["L0_ffn_W1"][h * H:(h + 1) * H].rearrange("e d f -> d e f")) for h in range(2)]
        ev_w2 = [load(f"w2_{h}", w2f[:, h * H * FC:(h + 1) * H * FC, :],
                      A["L0_ffn_W2"][h * H:(h + 1) * H].rearrange("e (c p) d -> p (e c) d", p=P))
                 for h in range(2)]

        def flat(name):
            return A[name].rearrange("e f -> (e f)")

        ev_b1 = load("b1", b1c[:, :], flat("L0_ffn_b1").rearrange("(p c) -> p c", p=P))
        ev_gb = [load(n, gb[q * NB:(q + 1) * NB, :], flat("L0_ffn_" + n).rearrange("(c p) -> c p", p=P))
                 for q, n in enumerate(("g1", "be1"))]
        ev_b2 = load("b2", b2row[:, :], flat("L0_ffn_b2").rearrange("(o n) -> o n", o=1))
        ev_g2 = load("g2", g2[:, :], flat("L0_ffn_g2").rearrange("(o n) -> o n", o=1).to_broadcast([P, E * D]))
        ev_be2 = load("be2", be2[:, :], flat("L0_ffn_be2").rearrange("(o n) -> o n", o=1).to_broadcast([P, E * D]))

        s_const = signal("constants")

        def const(issue, after=()):
            return pr.add("gpsimd", issue, after, s_const)

        const(lambda e: e.memset(ones[:, :], 1.0))
        const(lambda e: e.memset(ones16[:, :], 1.0))
        const(lambda e: e.memset(onesb[:, :], 1.0))
        const(lambda e: e.memset(mean_w[:, :], 1.0 / F))
        const(lambda e: e.memset(zero_rows[:, :], 0.0))
        const(lambda e: e.memset(filled[:, 0, :], 0.0))
        const(lambda e: e.iota(iota_e[:, :, :], [[0, GT], [1, E]], base=0, channel_multiplier=0,
                               allow_small_or_imprecise_dtypes=True))
        const(lambda e: e.iota(trash_row[:, :], [[P, SLOT_TILES]], base=0, channel_multiplier=1,
                               allow_small_or_imprecise_dtypes=True))
        const(lambda e: e.iota(home_row[:, :, :], [[TOKENS, K], [P, TILES]], base=TRASH,
                               channel_multiplier=1))
        const(lambda e: e.iota(slot_no[:, :], [[1, SLOT_TILES]], base=0, channel_multiplier=0,
                               allow_small_or_imprecise_dtypes=True))
        ev_reg0 = const(lambda e: e.iota(region0[:, :], [[REGION, E]], base=0, channel_multiplier=0,
                                         allow_small_or_imprecise_dtypes=True))
        const(lambda e: e.affine_select(out=ident[:, :], in_=ones[:, :], compare_op=ALU.is_equal, fill=0.0,
                                        base=0, pattern=[[-1, P]], channel_multiplier=1), [ev_reg0])
        const(lambda e: e.affine_select(out=ident16[:, :], in_=ones16[:, :], compare_op=ALU.is_equal,
                                        fill=0.0, base=0, pattern=[[-1, P]], channel_multiplier=1))
        const(lambda e: e.affine_select(out=below[:, :], in_=onesb[:, :], compare_op=ALU.is_gt, fill=0.0,
                                        base=0, pattern=[[1, P]], channel_multiplier=-1))
        const(lambda e: e.affine_select(out=tri[:, :, :], in_=ones[0:1, 0:E * E].rearrange(
            "p (a b) -> p a b", a=E), compare_op=ALU.is_ge, fill=0.0, base=0, pattern=[[1, E], [-1, E]],
            channel_multiplier=0))
        ev_const = const(lambda e: e.memset(b1t[:, :], 0.0))

        s_pw, s_cw = signal("pe_attn_weights"), signal("copied_attn_weights")

        def pe(issue, after, sig):
            return pr.add("tensor", issue, after, sig)

        def mm(dst, lhsT, rhs, start=True, stop=True):
            return lambda e: e.matmul(dst, lhsT, rhs, start=start, stop=stop)

        def tp(dst, src, idn):
            return lambda e: e.transpose(dst, src, idn)

        b0, b1_, b2_, b3 = bank[0:4]
        pe(tp(b0[:, 0:D], WO, ident[:, :]), [ev_const, ev_w4["Wo"]], s_pw)
        pe(mm(b0[:, D:2 * D], WK, WQ), [ev_w4["Wk"], ev_w4["Wq"]], s_pw)
        t = pe(mm(b0[:, 2 * D:2 * D + 1], WK, bcol[:, 0:1]), [ev_bq], s_pw)
        pr.add("vector", lambda e: e.tensor_copy(woT[:, :], b0[:, 0:D]), [t], s_cw)
        pr.add("vector", lambda e: e.tensor_copy(wkq[:, :], b0[:, D:2 * D]), [], s_cw)
        t = pr.add("vector", lambda e: e.tensor_copy(kb_col[:, :], b0[:, 2 * D:2 * D + 1]), [], s_cw)
        pe(mm(b1_[:, 0:D], WV, woT[:, :]), [t, ev_w4["Wv"]], s_pw)
        pe(mm(b1_[0:1, D:2 * D], bcol[:, 1:2], woT[:, :], stop=False), [ev_bv], s_pw)
        t = pe(mm(b1_[0:1, D:2 * D], ones[0:1, 0:1], borow[:, :], start=False), [ev_bo], s_pw)
        pr.add("vector", lambda e: e.tensor_copy(wvo[:, :], b1_[:, 0:D]), [t], s_cw)
        ev_wvo = pr.add("vector", lambda e: e.tensor_copy(vb_row[:, :], b1_[0:1, D:2 * D]), [], s_cw)
        s_ct, s_ctc = signal("pe_ctxT"), signal("copied_ctxT")
        halves = range(CTX_TILES * P // 512)
        ev_half = []
        for h in halves:
            for c in range(4):
                t = pe(tp(bank[2 + h][:, c * P:(c + 1) * P], cx[:, h * 4 + c, :], ident[:, :]), [ev_cx], s_ct)
            ev_half.append(pr.add("scalar", lambda e, h=h: e.activation(
                cxT[:, h * 512:(h + 1) * 512], bank[2 + h][:, :], ACT.Copy), [t], s_ctc))
        s_kq, s_kqc = signal("pe_keys"), signal("copied_keys")
        for h in halves:
            cols = slice(h * 512, (h + 1) * 512)
            t = pe(mm(bank[4 + h][:, :], wkq[:, :], cxT[:, cols]), [ev_half[h]], s_kq)
            pr.add("vector", lambda e, h=h, cols=cols: e.tensor_copy(kq[:, cols], bank[4 + h][:, :]),
                   [t], s_kqc)
            t = pe(mm(bank[6 + h][0:1, :], kb_col[:, :], cxT[:, cols]), [], s_kq)
            ev_kq = pr.add("vector", lambda e, h=h, cols=cols: e.tensor_copy(
                kb_row[:, cols], bank[6 + h][0:1, :]), [t], s_kqc)
        s_vo, s_voc = signal("pe_values"), signal("copied_values")
        for h in halves:
            for c in range(4):
                n = h * 4 + c
                pe(mm(bank[2 + h][:, c * P:(c + 1) * P], cxT[:, n * P:(n + 1) * P], wvo[:, :], stop=False),
                   [ev_wvo, ev_half[h]], s_vo)
                t = pe(mm(bank[2 + h][:, c * P:(c + 1) * P], ones[0:1, :], vb_row[:, :], start=False),
                       [], s_vo)
            ev_vo = pr.add("scalar", lambda e, h=h: e.activation(
                vo[:, h * 4:(h + 1) * 4, :], bank[2 + h][:, :].rearrange("p (c d) -> p c d", c=4), ACT.Copy),
                [t], s_voc)

        s = {n: signal(n) for n in (
            "stats", "ve", "lnv", "newton", "xn", "pe_xnT", "xnT", "pe_score", "smax", "prob", "rsum",
            "pe_pT", "pT", "pe_attn", "x2", "xt", "pe_xtT", "xtT", "pe_logit", "logit", "top", "pay_hi",
            "pay_lo", "pay_copy", "pay_home", "pe_rank", "rank", "pos", "scatter0", "scatter1")}
        done = {}

        def vec(key, issue, after=()):
            return pr.add("vector", issue, after, s[key])

        def act(key, issue, after=()):
            return pr.add("scalar", issue, after, s[key])

        def norm_stats(g, n, src, after):
            for i in range(GT):
                t = vec("stats", lambda e, i=i: e.bn_stats(st[:, n, i, :], src(i)), after)
            for i in range(GT):
                t2 = vec("stats", lambda e, i=i: e.bn_aggr(mv[:, n, i, :], st[:, n, i, :]), [t])
            t = vec("ve", lambda e: e.tensor_scalar(ve[:, n, :], mv[:, n, :, 1], EPS, None, ALU.add), [t2])
            t = act("lnv", lambda e: e.activation(lnv[:, n, :], ve[:, n, :], ACT.Ln), [t])
            t = act("lnv", lambda e: e.activation(y0[:, n, :], lnv[:, n, :], ACT.Exp, scale=-0.5), [t])
            t = vec("newton", lambda e: e.tensor_tensor(yy[:, n, :], y0[:, n, :], y0[:, n, :], ALU.mult), [t])
            t = vec("newton", lambda e: e.tensor_tensor(yv[:, n, :], yy[:, n, :], ve[:, n, :], ALU.mult), [t])
            t = vec("newton", lambda e: e.tensor_scalar(yt[:, n, :], yv[:, n, :], -0.5, 1.5, ALU.mult,
                                                        ALU.add), [t])
            return vec("newton", lambda e: e.tensor_tensor(rstd[:, n, :], y0[:, n, :], yt[:, n, :],
                                                           ALU.mult), [t])

        def a_norm(g):
            t = norm_stats(g, 0, lambda i: x[:, g * GT + i, :], [ev_x[g]])
            for i in range(GT):
                done["xn", g] = vec("xn", lambda e, i=i: e.tensor_scalar(
                    xn[:, i, :], x[:, g * GT + i, :], mv[:, 0, i, 0:1], rstd[:, 0, i:i + 1], ALU.subtract,
                    ALU.mult), [t, done.get(("pe_xnT", g - 1))])

        def a_xnT(g):
            for i in range(GT):
                t = pe(tp(bank[0][:, i * P:(i + 1) * P], xn[:, i, :], ident[:, :]),
                       [done["xn", g], done.get(("xnT", g - 1))], s["pe_xnT"])
            done["pe_xnT", g] = t
            done["xnT", g] = act("xnT", lambda e: e.activation(xnT[:, :], bank[0][:, :], ACT.Copy),
                                 [t, done.get(("pe_score", g - 1))])

        def a_score(g):
            for i in range(GT):
                b, q = i // 2, i % 2
                keys = slice((2 * g + b) * KEYS, (2 * g + b + 1) * KEYS)
                dst = bank[1][:, (2 * q + b) * KEYS:(2 * q + b + 1) * KEYS]
                pe(mm(dst, xnT[:, i * P:(i + 1) * P], kq[:, keys], stop=False),
                   [done["xnT", g], ev_kq, done.get(("prob", g - 1))], s["pe_score"])
                t = pe(mm(dst, ones[0:1, :], kb_row[:, keys], start=False), [], s["pe_score"])
            done["pe_score", g] = t
            sv = bank[1][:, 0:4 * KEYS].rearrange("p (q b k) -> p q b k", q=2, b=2)
            t = vec("smax", lambda e: e.tensor_reduce(smax[:, :, :], sv, AX.X, ALU.max),
                    [t])
            t = vec("smax", lambda e: e.tensor_scalar(nmax[:, :, :], smax[:, :, :], -SCALE, None, ALU.mult),
                    [t, done.get(("prob", g - 1))])
            for q in range(2):
                for b in range(2):
                    t2 = act("prob", lambda e, q=q, b=b: e.activation(
                        prob[:, q, b, :], sv[:, q, b, :], ACT.Exp, bias=nmax[:, q, b:b + 1], scale=SCALE,
                        accum_out=psum_[:, q, b:b + 1]),
                        [t, done.get(("pe_pT", g - 1)), done.get(("rsum", g - 1))])
            done["prob", g] = t2
            done["rsum", g] = vec("rsum", lambda e: e.reciprocal(rsum[:, :, :], psum_[:, :, :]), [t2, done.get(("x2", g - 1))])

        def a_attend(g):
            for q in range(2):
                t = pe(tp(bank[2][:, q * P:(q + 1) * P],
                          prob[:, q, :, :].rearrange("p b k -> p (b k)"), ident[:, :]),
                       [done["prob", g], ev_vo, done.get(("pT", g - 1))], s["pe_pT"])
            done["pe_pT", g] = t
            done["pT", g] = act("pT", lambda e: e.activation(
                pT[:, :, :], bank[2][:, 0:2 * P].rearrange("p (q k) -> p q k", q=2), ACT.Copy),
                [t, done.get(("pe_attn", g - 1))])
            def attn(b, q):
                return bank[3 + 4 * b][:, q * D:(q + 1) * D]

            for i in range(GT):
                b, q = i // 2, i % 2
                rows = slice(b * KEYS, (b + 1) * KEYS)
                t = pe(mm(attn(b, q), pT[rows, q, :], vo[rows, g, :]),
                       [done["pT", g], ev_kq, done.get(("x2", g - 1))], s["pe_attn"])
            done["pe_attn", g] = t
            for i in range(GT):
                b, q = i // 2, i % 2
                done["x2", g] = vec("x2", lambda e, i=i, b=b, q=q: e.scalar_tensor_tensor(
                    out=x2[:, g * GT + i, :], in0=attn(b, q), scalar=rsum[:, q, b:b + 1],
                    in1=x[:, g * GT + i, :], op0=ALU.mult, op1=ALU.add), [t, done["rsum", g]])

        def a_norm2(g):
            t = norm_stats(g, 1, lambda i: x2[:, g * GT + i, :], [done["x2", g]])
            for i in range(GT):
                done["xt", g] = vec("xt", lambda e, i=i: e.tensor_scalar(
                    xt[:, i, :], x2[:, g * GT + i, :], mv[:, 1, i, 0:1], rstd[:, 1, i:i + 1], ALU.subtract,
                    ALU.mult), [t, done.get(("pe_xtT", g - 1)), done.get(("pay_hi", g - 1)),
                                done.get(("pay_lo", g - 1))])

        def a_logits(g):
            for i in range(GT):
                t = pe(tp(bank[4][:, i * P:(i + 1) * P], xt[:, i, :], ident[:, :]),
                       [done["xt", g], done.get(("xtT", g - 1))], s["pe_xtT"])
            done["pe_xtT", g] = t
            done["xtT", g] = act("xtT", lambda e: e.activation(xtT[:, :], bank[4][:, :], ACT.Copy),
                                 [t, done.get(("pe_logit", g - 1))])
            for i in range(GT):
                dst = bank[5][:, i * E:(i + 1) * E]
                pe(mm(dst, xtT[:, i * P:(i + 1) * P], wr[:, :], stop=False),
                   [done["xtT", g], ev_wr, ev_br, done.get(("rank", g - 1))], s["pe_logit"])
                t = pe(mm(dst, ones[0:1, :], brrow[:, :], start=False), [], s["pe_logit"])
            done["pe_logit", g] = t
            done["logit", g] = vec("logit", lambda e: e.tensor_copy(
                lg[:, :, :], bank[5][:, 0:GT * E].rearrange("p (i e) -> p i e", i=GT)), [t])

        def a_payload(g):
            p = pay[g % 2]
            free = [done.get(("scatter", g - 2))]
            t = act("pay_hi", lambda e: e.activation(p[:, 0, :, 0:D], xt[:, :, :], ACT.Copy),
                    [done["xt", g], *free])
            done["pay_hi", g] = t
            t = vec("pay_lo", lambda e: e.tensor_tensor(p[:, 0, :, D:2 * D], xt[:, :, :], p[:, 0, :, 0:D],
                                                        ALU.subtract), [t])
            done["pay_lo", g] = t
            vec("pay_copy", lambda e: e.tensor_copy(
                p[:, :, :, 2 * D:2 * D + 2].bitcast(U32)[:, :, :, 0], home_row[:, :, g * GT:(g + 1) * GT]),
                [ev_const, *free])
            done["pay", g] = vec("pay_copy", lambda e: e.tensor_copy(
                p[:, 1, :, 0:2 * D], p[:, 0, :, 0:2 * D]), [t])

        def a_route(g):
            for i in range(GT):
                t = vec("top", lambda e, i=i: e.max(top[:, g * GT + i, :], lg[:, i, :]), [done["logit", g]])
            for i in range(GT):
                t2 = vec("top", lambda e, i=i: e.max_index(topi[:, i, :], top[:, g * GT + i, :], lg[:, i, :]),
                         [t])
            for k in range(K):
                t = vec("top", lambda e, k=k: e.tensor_tensor(
                    oh[:, k, :, :], iota_e[:, :, :], topi[:, :, k:k + 1].to_broadcast([P, GT, E]),
                    ALU.is_equal), [t2, ev_const])
            t = vec("top", lambda e: e.tensor_tensor(mask[:, :, :], oh[:, 0, :, :], oh[:, 1, :, :], ALU.add),
                    [t])
            m = mask[:, :, :].rearrange("p i e -> p (i e)")
            pe(mm(bank[5][:, 64:64 + GT * E], below[:, :], m, stop=False), [t], s["pe_rank"])
            for d in range(1, GT):
                pe(mm(bank[5][:, 64 + d * E:64 + GT * E], onesb[:, :], m[:, 0:(GT - d) * E], start=False,
                      stop=(d == GT - 1)), [], s["pe_rank"])
            for i in range(GT):
                t = pe(mm(bank[5][:, 128:128 + E], onesb[:, :], m[:, i * E:(i + 1) * E], start=(i == 0),
                          stop=(i == GT - 1)), [], s["pe_rank"])
            c, nx = g % 2, (g + 1) % 2
            vec("rank", lambda e: e.tensor_tensor(
                rank[:, :, :], bank[5][:, 64:64 + GT * E].rearrange("p (i e) -> p i e", i=GT),
                filled[:, c:c + 1, :].to_broadcast([P, GT, E]), ALU.add), [t, done.get(("rank", g - 1))])
            done["rank", g] = t = vec("rank", lambda e: e.tensor_tensor(
                filled[:, nx, :], bank[5][:, 128:128 + E], filled[:, c, :], ALU.add))
            t = vec("pos", lambda e: e.tensor_tensor(
                rank[:, :, :], rank[:, :, :],
                region0[:, :].rearrange("p (i e) -> p i e", i=1).to_broadcast([P, GT, E]), ALU.add), [t])
            for k in range(K):
                t2 = vec("pos", lambda e, k=k: e.tensor_tensor(pick[:, k, :, :], oh[:, k, :, :],
                                                               rank[:, :, :], ALU.mult), [t])
            t = vec("pos", lambda e: e.tensor_reduce(posf[:, :, :], pick[:, :, :, :], AX.X, ALU.add), [t2])
            t = vec("pos", lambda e: e.tensor_copy(pos[:, g % 2, :, :], posf[:, :, :]),
                    [t, done.get(("scatter", g - 2))])
            for k in range(K):
                for i in range(GT):
                    done["scatter", g] = pr.add("gpsimd", lambda e, k=k, i=i: e.indirect_dma_start(
                        slots, bass.IndirectOffsetOnAxis(ap=pos[:, g % 2, k, i:i + 1], axis=0),
                        pay[g % 2][:, k, i, :], None), [t, done["pay", g]],
                        s[f"scatter{g % 2}"], 16)

        s_scale, s_sp = signal("scale"), signal("pe_scale")

        def weight_scale():
            def top_abs(col, src, after):
                return pr.add("vector", lambda e: e.tensor_reduce(
                    mx[:, col:col + 1], src, AX.X, ALU.max, apply_absolute_value=True), after, s_scale)
            t = pe(tp(bank[6][:, 0:2 * NB], gb[:, :], ident[0:2 * NB, 0:2 * NB]), [*ev_gb, ev_kq], s_sp)
            ev_g1 = pr.add("vector", lambda e: e.tensor_copy(gbT[:, :], bank[6][:, 0:2 * NB]), [t], s_scale)
            top_abs(0, w1f[:, :], ev_w1)
            top_abs(1, b1c[:, :], [ev_b1])
            top_abs(2, w2f[:, :, :].rearrange("p c d -> p (c d)"), ev_w2)
            t = top_abs(3, g1c[:, :], [ev_g1])
            t = pe(tp(bank[6][0:4, 0:P], mx[:, :], ident[:, :]), [t, ev_kq], s_sp)

            def dv(issue, after):
                return pr.add("vector", issue, after, s_scale)
            t = dv(lambda e: e.tensor_reduce(mx4[:, :], bank[6][0:4, 0:P], AX.X, ALU.max), [t])
            t = dv(lambda e: e.tensor_scalar(dg4[:, :], ident[0:4, 0:4], mx4[:, 0:1], None, ALU.mult), [t])
            t = pe(mm(bank[6][:, 128:132], ones[0:4, :], dg4[:, :]), [t], s_sp)
            t = dv(lambda e: e.tensor_copy(mb[:, :], bank[6][:, 128:132]), [t])
            done["scale_bank"] = t
            dv(lambda e: e.tensor_tensor(mm2[:, 0:1], mb[:, 0:1], mb[:, 1:2], ALU.max), [t])
            t = dv(lambda e: e.scalar_tensor_tensor(out=mm2[:, 1:2], in0=mb[:, 2:3], scalar=2.0,
                                                    in1=mb[:, 3:4], op0=ALU.mult, op1=ALU.mult), [])
            t = dv(lambda e: e.tensor_scalar(mb[:, 0:2], mm2[:, :], 1e-30, 1e30, ALU.max, ALU.min), [t])
            t = dv(lambda e: e.tensor_scalar(pw2[:, :], mb[:, 0:2].bitcast(U32), 0x7F800000, None,
                                             ALU.bitwise_and), [t])
            t = dv(lambda e: e.reciprocal(scg[:, :], pw2[:, :].bitcast(F32)), [t])
            t = dv(lambda e: e.tensor_scalar(sc[:, :], scg[:, :], GUARD, None, ALU.mult), [t])
            t = dv(lambda e: e.tensor_tensor(sc2[:, :], sc[:, :], sc[:, :], ALU.mult), [t])
            done["scale"] = dv(lambda e: e.tensor_scalar(epsS[:, :], sc2[:, :], EPS, None, ALU.mult), [t])
            t = dv(lambda e: e.tensor_scalar(b1h[:, :], b1c[:, :], sc[:, 0:1], None, ALU.mult),
                   [done["scale"]])
            t = dv(lambda e: e.scalar_tensor_tensor(out=b1l[:, :], in0=b1c[:, :], scalar=sc[:, 0:1],
                                                    in1=b1h[:, :], op0=ALU.mult, op1=ALU.subtract), [t])
            s_b1 = signal("b1_rows")
            for n, src in enumerate((b1h, b1l)):
                done["b1t"] = pr.add("sync", lambda e, n=n, src=src: e.dma_start(
                    b1t[n:n + 1, :].rearrange("o (p c) -> o p c", p=P), src[:, :]), [t, ev_const], s_b1, 16)

        s_w = {n: signal(n) for n in ("w_hi", "w_lo", "w2g", "w2c", "pe_w2", "c2row", "pe_c2", "c2")}

        def expert_weights(e_):
            cols = slice(e_ * F, (e_ + 1) * F)
            pair = lambda t: t[:, cols]
            t = pr.add("scalar", lambda e: e.activation(pair(w1h), pair(w1f), ACT.Copy, scale=sc[:, 0:1]),
                       [done["scale"]], s_w["w_hi"])
            pr.add("vector", lambda e: e.scalar_tensor_tensor(
                out=pair(w1l), in0=pair(w1f), scalar=sc[:, 0:1], in1=pair(w1h), op0=ALU.mult,
                op1=ALU.subtract), [t], s_w["w_lo"])
            for c in range(FC):
                n = e_ * FC + c
                t = pr.add("vector", lambda e, n=n, c=c: e.tensor_scalar(
                    w2g[:, c, :], w2f[:, n, :], g1c[:, n:n + 1], sc[:, 1:2], ALU.mult, ALU.mult),
                    [done.get(("pe_w2", e_ - 1)), done.get(("w2c", e_ - 1))], s_w["w2g"])
            for c in range(FC):
                t2 = pe(mm(bank[6][:, 0:D], mean_w[:, :], w2g[:, c, :], start=(c == 0), stop=(c == FC - 1)),
                        [t, done["scale_bank"], done.get(("w2c", e_ - 1)), done.get(("c2row", e_ - 1))], s_w["pe_w2"])
            done["w2c", e_] = t3 = pr.add("vector", lambda e: e.tensor_tensor(
                w2c[:, :, :], w2g[:, :, :],
                bank[6][:, 0:D].rearrange("p (c d) -> p c d", c=1).to_broadcast([P, FC, D]), ALU.subtract),
                [t2, done.get(("w_lo2", e_ - 1))], s_w["w2c"])
            for c in range(FC):
                n = e_ * FC + c
                pe(mm(bank[6][0:1, 128:128 + D], be1c[:, n:n + 1], w2f[:, n, :], start=(c == 0), stop=False),
                   [t3], s_w["pe_w2"])
            t2 = pe(mm(bank[6][0:1, 128:128 + D], ones[0:1, 0:1], b2row[:, e_ * D:(e_ + 1) * D],
                       start=False), [ev_b2], s_w["pe_w2"])
            done["pe_w2", e_] = t2
            done["c2row", e_] = pr.add("vector", lambda e: e.tensor_scalar(
                c2row[:, e_ * D:(e_ + 1) * D], bank[6][0:1, 128:128 + D], sc[0:1, 1:2], None, ALU.mult),
                [t2], s_w["c2row"])
            wv = lambda t: t[:, cols].rearrange("p (c d) -> p c d", c=FC)
            t = pr.add("scalar", lambda e: e.activation(wv(w2h), w2c[:, :, :], ACT.Copy), [t3],
                       s_w["w_hi"])
            done["w_lo2", e_] = pr.add("vector", lambda e: e.tensor_tensor(
                wv(w2l), w2c[:, :, :], wv(w2h), ALU.subtract), [t], s_w["w_lo"])
            if e_ == E - 1:
                for h in range(E * D // 512):
                    hc = slice(h * 512, (h + 1) * 512)
                    t = pe(mm(bank[7][:, :], ones[0:1, :], c2row[:, hc]),
                           [done["c2row", e_], done["x2", GROUPS - 1], done.get("c2")], s_w["pe_c2"])
                    done["c2"] = pr.add("scalar", lambda e, hc=hc: e.activation(
                        c2[:, hc], bank[7][:, :], ACT.Copy), [t], s_w["c2"])

        stages = [a_norm, a_xnT, a_score, a_attend, a_norm2, a_logits, a_payload, a_route]
        OFF = [0, 0, 0, 1, 1, 1, 1, 1]
        for step in range(GROUPS + max(OFF)):
            for f, o in sorted(zip(stages, OFF), key=lambda fo: -fo[1]):
                if 0 <= step - o < GROUPS:
                    f(step - o)
            if step == 1:
                weight_scale()
        for e_ in range(E):
            expert_weights(e_)

        s_tab = signal("tables")

        def tab(issue, after=()):
            return pr.add("vector", issue, after, s_tab)

        fin = GROUPS % 2
        last = done["rank", GROUPS - 1]
        t = tab(lambda e: e.tensor_tensor(tailf[:, :], filled[0:1, fin, :], region0[0:1, :], ALU.add), [last])
        ev_tail = tab(lambda e: e.tensor_copy(tail[:, :], tailf[:, :]), [t])
        t = tab(lambda e: e.tensor_scalar(cnti[:, :], filled[0:1, fin, :], float(P - 1), None, ALU.add))
        t = tab(lambda e: e.tensor_scalar(nti[:, :], cnti[:, :], P.bit_length() - 1, None,
                                          ALU.arith_shift_right), [t])
        t = tab(lambda e: e.tensor_copy(ntf[:, :], nti[:, :]), [t])
        as_row = lambda ap, n: ap.rearrange("p (a e) -> p a e", a=1).to_broadcast([1, n, E])
        t = tab(lambda e: e.tensor_tensor(ntri[:, :, :], tri[:, :, :], as_row(ntf[:, :], E), ALU.mult), [t])
        t = tab(lambda e: e.tensor_reduce(cum[:, :], ntri[:, :, :], AX.X, ALU.add), [t])
        t = tab(lambda e: e.tensor_tensor(
            full[:, :, :], as_row(cum[:, :], SLOT_TILES),
            slot_no[:, :].rearrange("p (j a) -> p j a", a=1).to_broadcast([1, SLOT_TILES, E]), ALU.is_le), [t])
        tab(lambda e: e.tensor_reduce(sx[:, :], full[:, :, :], AX.X, ALU.add), [t])
        t = tab(lambda e: e.tensor_tensor(fulln[:, :, :], full[:, :, :], as_row(ntf[:, :], SLOT_TILES),
                                          ALU.mult))
        t = tab(lambda e: e.tensor_reduce(sfirst[:, :], fulln[:, :, :], AX.X, ALU.add), [t])
        t = tab(lambda e: e.tensor_tensor(sa[:, :], slot_no[:, :], sfirst[:, :], ALU.subtract), [t])
        t = tab(lambda e: e.tensor_scalar(sb_[:, :], sx[:, :], float(REGION), None, ALU.mult), [t])
        t = tab(lambda e: e.scalar_tensor_tensor(out=sa[:, :], in0=sa[:, :], scalar=float(P), in1=sb_[:, :],
                                                 op0=ALU.mult, op1=ALU.add), [t])
        tab(lambda e: e.tensor_scalar(row_tab[:, :], sa[:, :], float(E * REGION), None, ALU.min), [t])
        t = tab(lambda e: e.tensor_scalar(smin[:, :], sx[:, :], float(E - 1), None, ALU.min))
        tab(lambda e: e.tensor_scalar(off_w[:, :], smin[:, :], float(F), None, ALU.mult), [t])
        ev_tab = tab(lambda e: e.tensor_scalar(off_d[:, :], smin[:, :], float(D), None, ALU.mult), [t])

        s_zero = signal("zeroed")

        def zero_tail(e_):
            def issue(eng):
                row = eng.value_load(tail[0:1, e_:e_ + 1], min_val=e_ * REGION, max_val=e_ * REGION + TOKENS)
                return eng.dma_start(slots[bass.ds(row, P), :], zero_rows[:, :])
            return issue

        for e_ in range(E):
            pr.add("sync", zero_tail(e_), [ev_tail, ev_const], s_zero, 16)
        ev_zero = pr.add("sync", lambda e: e.dma_start(slots[E * REGION:, :], zero_rows[:, :]), [], s_zero, 16)

        s.update({n: signal(n) for n in (
            "pe_xsT", "xsT", "pe_h", "relu1", "bstats1", "std1", "rstd1", "pe_rT", "rT_hi", "rT_lo", "pe_y",
            "affine", "relu2", "bstats2", "std2", "rstd2", "z", "z_out", "dest", "answer")})
        s_rows = [signal(f"rows{n}") for n in range(NX)]
        s_ans = [signal(f"answer{n}") for n in range(NZ)]
        scattered = [done["scatter", GROUPS - 1], done["scatter", GROUPS - 2]]
        psX, psH, psT, psY = bank[0:2], bank[2:4], bank[4:6], bank[6:8]
        W_MAX, D_MAX = (E - 1) * F, (E - 1) * D
        regs = {}

        def b_load(j):
            def issue(eng):
                row = eng.value_load(row_tab[0:1, j:j + 1], min_val=0, max_val=E * REGION)
                return eng.dma_start(xs[j % NX][:, :], slots[bass.ds(row, P), :])
            done["rows", j] = pr.add("sync", issue, [ev_tab, ev_zero, *scattered,
                                                     done.get(("pe_xsT", j - NX)), done.get(("dest", j - NX))],
                                     s_rows[j % NX], 16)

        def b_turn(j):
            v = psX[j % 2][:, 0:P].bitcast(F16)
            for n in range(2):
                t = pe(tp(v[:, n * P:(n + 1) * P], xs[j % NX][:, n * D:(n + 1) * D], ident16[:, :]),
                       [done["rows", j], done.get(("xsT", j - 2)), done.get("phase")], s["pe_xsT"])
            done["pe_xsT", j] = t
            done["xsT", j] = act("xsT", lambda e: e.activation(xsT[j % 2][:, :], v, ACT.Copy),
                                 [t, done.get(("pe_h", j - 2))])

            done["dest", j] = vec("dest", lambda e: e.tensor_tensor(
                dest[j % ND][:, :], xs[j % NX][:, 2 * D:2 * D + 2].bitcast(U32), trash_row[:, j:j + 1],
                ALU.max), [done["rows", j], done.get(("answer", j - ND))])

        def b_up(j):
            hi, lo = xsT[j % 2][:, 0:P], xsT[j % 2][:, P:2 * P]
            dst = psH[j % 2][:, :]

            def issue(eng):
                off = regs["pe", j] = eng.value_load(off_w[0:1, j:j + 1], min_val=0, max_val=W_MAX)
                w = lambda t: t[:, bass.ds(off, F)]
                eng.matmul(dst, ones16[:, :], w(b1t), start=True, stop=False)
                eng.matmul(dst, hi, w(w1h), start=False, stop=False)
                eng.matmul(dst, hi, w(w1l), start=False, stop=False)
                return eng.matmul(dst, lo, w(w1h), start=False, stop=True)
            done["pe_h", j] = pe(issue, [done["xsT", j], done.get(("relu1", j - 2)), done["b1t"],
                                         done["w_lo2", E - 1], ev_tab], s["pe_h"])
            done["relu1", j] = act("relu1", lambda e: e.activation(r[j % 2][:, :], dst, ACT.Relu),
                                   [done["pe_h", j], done.get(("pe_rT", j - 2)), done.get(("bstats1", j - 2))])

        def b_stats(j):
            n = j % 4
            t = vec("bstats1", lambda e: e.bn_stats(st1[n][:, :], r[j % 2][:, :]), [done["relu1", j]])
            done["bstats1", j] = t
            t = vec("bstats1", lambda e: e.bn_aggr(mv1[n][:, :], st1[n][:, :]), [t])
            t = act("std1", lambda e: e.activation(sd1[n][:, :], mv1[n][:, 1:2], ACT.Sqrt, bias=epsS[:, 0:1]),
                    [t])
            done["rstd1", j] = vec("rstd1", lambda e: e.reciprocal(rs1[n][:, :], sd1[n][:, :]), [t])

        def b_turn_r(j):
            for c in range(FC):
                t = pe(tp(psT[j % 2][:, c * P:(c + 1) * P], r[j % 2][:, c * P:(c + 1) * P], ident[:, :]),
                       [done["relu1", j], done.get(("rT_lo", j - 2))], s["pe_rT"])
            done["pe_rT", j] = t
            t = act("rT_hi", lambda e: e.activation(rTh[j % 2][:, :], psT[j % 2][:, :], ACT.Copy),
                    [t, done.get(("pe_y", j - 2))])
            done["rT_lo", j] = vec("rT_lo", lambda e: e.tensor_tensor(
                rTl[j % 2][:, :], psT[j % 2][:, :], rTh[j % 2][:, :], ALU.subtract), [t])

        def b_down(j):
            dst = psY[j % 2][:, 0:D]

            def issue(eng):
                off = regs["pe", j]
                for c in range(FC):
                    hi, lo = (t[j % 2][:, c * P:(c + 1) * P] for t in (rTh, rTl))
                    wh, wl = (t[:, bass.ds(off + c * D, D)] for t in (w2h, w2l))
                    eng.matmul(dst, hi, wh, start=(c == 0), stop=False)
                    eng.matmul(dst, hi, wl, start=False, stop=False)
                    ins = eng.matmul(dst, lo, wh, start=False, stop=(c == FC - 1))
                return ins
            done["pe_y", j] = pe(issue, [done["rT_lo", j], done.get(("affine", j - 2))], s["pe_y"])

        def b_affine(j):
            n = j % 4

            def issue(eng):
                off = eng.value_load(off_d[0:1, j:j + 1], min_val=0, max_val=D_MAX)
                return eng.scalar_tensor_tensor(out=u[j % 3][:, :], in0=psY[j % 2][:, 0:D],
                                                scalar=rs1[n][:, 0:1], in1=c2[:, bass.ds(off, D)],
                                                op0=ALU.mult, op1=ALU.add)
            t = done["affine", j] = vec("affine", issue, [done["pe_y", j], done["rstd1", j], done["c2"],
                                                          done.get(("relu2", j - 3))])
            t = act("relu2", lambda e: e.activation(ur[j % 3][:, :], u[j % 3][:, :], ACT.Relu),
                    [t, done.get(("z", j - 3))])
            done["relu2", j] = t

        def b_stats2(j):
            n = j % 4
            t = vec("bstats2", lambda e: e.bn_stats(st2[n][:, :], ur[j % 3][:, :]), [done["relu2", j]])
            t = vec("bstats2", lambda e: e.bn_aggr(mv2[n][:, :], st2[n][:, :]), [t, done.get(("z", j - 4))])
            t = act("std2", lambda e: e.activation(sd2[n][:, :], mv2[n][:, 1:2], ACT.Sqrt, bias=epsS[:, 1:2]),
                    [t])
            done["rstd2", j] = vec("rstd2", lambda e: e.reciprocal(rs2[n][:, :], sd2[n][:, :]), [t])

        def b_out(j):
            n = j % 4
            pool = lambda issue, after=(): pr.add("gpsimd", issue, after, s["z"])
            t = pool(lambda e: e.tensor_scalar(z0[j % 2][:, :], ur[j % 3][:, :], mv2[n][:, 0:1],
                                               rs2[n][:, 0:1], ALU.subtract, ALU.mult), [done["rstd2", j]])
            done["z", j] = t

            def scaled(eng):
                off = regs["pool", j] = eng.value_load(off_d[0:1, j:j + 1], min_val=0, max_val=D_MAX)
                return eng.tensor_tensor(z1[j % 2][:, :], z0[j % 2][:, :], g2[:, bass.ds(off, D)], ALU.mult)
            t = pool(scaled, [t, ev_g2, ev_be2, ev_tab])
            t = pool(lambda e: e.tensor_tensor(z[j % NZ][:, :], z1[j % 2][:, :],
                                               be2[:, bass.ds(regs["pool", j], D)], ALU.add),
                     [t, done.get(("answer", j - NZ))])
            done["answer", j] = pr.add("gpsimd", lambda e: e.indirect_dma_start(
                answers, bass.IndirectOffsetOnAxis(ap=dest[j % ND][:, 0:1], axis=0), z[j % NZ][:, :], None),
                [t, done["dest", j]], s_ans[j % NZ], 16)

        s_g = signal("gates")
        t = pr.add("vector", lambda e: e.tensor_tensor(gd[:, :], top[:, :, 1], top[:, :, 0], ALU.subtract),
                   [last], s_g)
        s_ge = signal("gate_exp")
        t = pr.add("scalar", lambda e: e.activation(ge_[:, :], gd[:, :], ACT.Exp), [t], s_ge)
        t = pr.add("vector", lambda e: e.tensor_scalar(gs[:, :], ge_[:, :], 1.0, None, ALU.add), [t], s_g)
        t = pr.add("vector", lambda e: e.reciprocal(gate[:, 0, :], gs[:, :]), [t], s_g)
        ev_gate = pr.add("vector", lambda e: e.tensor_tensor(gate[:, 1, :], ge_[:, :], gate[:, 0, :],
                                                             ALU.mult), [t], s_g)
        done["phase"] = ev_gate

        for j in range(NX):
            b_load(j)
        b_stages = [(b_out, 6), (b_stats2, 5), (b_affine, 4), (b_down, 3), (b_turn_r, 2), (b_stats, 2),
                    (b_up, 1), (b_turn, 0)]
        for step in range(SLOT_TILES + 6):
            for f, o in b_stages:
                j = step - o
                if 0 <= j < SLOT_TILES:
                    f(j)
                    if f is b_turn and j + NX < SLOT_TILES:
                        b_load(j + NX)

        s_ya = [signal(f"back{n}") for n in range(2)]
        s_c = signal("combined")
        s_out = [signal(f"stored{n}") for n in range(2)]
        answered = [done["answer", SLOT_TILES - 1 - n] for n in range(NZ)]
        for g in range(GROUPS):
            tiles = slice(g * GT, (g + 1) * GT)
            for k in range(K):
                t = pr.add("sync", lambda e, k=k, g=g: e.dma_start(
                    ya[g % 2][:, k, :, :], ans_v[:, k * TILES + g * GT:k * TILES + (g + 1) * GT, :]),
                    [*answered, done.get(("comb", g - 2))], s_ya[g % 2], 16)
            for i in range(GT):
                n = g * GT + i
                t1 = pr.add("vector", lambda e, g=g, i=i, n=n: e.scalar_tensor_tensor(
                    out=acc[g % 2][:, i, :], in0=ya[g % 2][:, 0, i, :], scalar=gate[:, 0, n:n + 1],
                    in1=x2[:, n, :], op0=ALU.mult, op1=ALU.add), [t, ev_gate], s_c)
            for i in range(GT):
                n = g * GT + i
                t2 = pr.add("vector", lambda e, g=g, i=i, n=n: e.scalar_tensor_tensor(
                    out=res[g % 2][:, i, :], in0=ya[g % 2][:, 1, i, :], scalar=gate[:, 1, n:n + 1],
                    in1=acc[g % 2][:, i, :], op0=ALU.mult, op1=ALU.add), [t1, done.get(("out", g - 2))], s_c)
            done["comb", g] = t2
            done["out", g] = pr.add("scalar", lambda e, g=g, tiles=tiles: e.dma_start(
                out_v[:, tiles, :], res[g % 2][:, :, :]), [t2], s_out[g % 2], 16)

        final = [done["out", GROUPS - 1], done["out", GROUPS - 2], ev_zero, *scattered, *answered]

        block = ctx.enter_context(nc.Block())
        for name in ("sync", "gpsimd", "scalar", "tensor", "vector"):
            def body(eng, name=name):
                for run in pr.queues[name]:
                    run(eng)
                if name == "sync":
                    for sig, value in final:
                        eng.wait_ge(sig.handle, value)
            {"sync": block.sync, "gpsimd": block.gpsimd, "scalar": block.scalar, "tensor": block.tensor,
             "vector": block.vector}[name](body)


_INS = ["x", "ctx_1024", "L0_xattn_Wk", "L0_xattn_Wv", "L0_xattn_bv", "L0_xattn_Wq", "L0_xattn_bq",
        "L0_xattn_Wo", "L0_xattn_bo", "L0_ffn_Wr", "L0_ffn_br", "L0_ffn_W1", "L0_ffn_b1", "L0_ffn_g1",
        "L0_ffn_be1", "L0_ffn_W2", "L0_ffn_b2", "L0_ffn_g2", "L0_ffn_be2"]


def kernel(**inputs):
    import concourse.bacc as bacc
    from concourse.bass_utils import run_bass_kernel_spmd

    nc = bacc.Bacc("TRN2", target_bir_lowering=False, num_devices=1)
    arrays, args = {}, {}
    for name in _INS:
        a = np.ascontiguousarray(inputs[name])
        arrays[f"in_{name}"] = a
        args[name] = nc.dram_tensor(f"in_{name}", a.shape, mybir.dt.from_np(a.dtype),
                                    kind="ExternalInput").ap()
    out = nc.dram_tensor("out_0", inputs["x"].shape, mybir.dt.float32, kind="ExternalOutput").ap()
    build(nc, args, out)
    r = run_bass_kernel_spmd(nc, [arrays], core_ids=[0])
    return r.results[0]["out_0"]
```

```python
import concourse.bass as bass
import numpy as np
from concourse import mybir
from contextlib import ExitStack

F32, F16, BF16, U32, I32 = (mybir.dt.float32, mybir.dt.float16, mybir.dt.bfloat16, mybir.dt.uint32,
                            mybir.dt.int32)
ALU = mybir.AluOpType
ACT = mybir.ActivationFunctionType
AX = mybir.AxisListType


class Signal:

    def __init__(self, handle):
        self.handle, self.count = handle, 0


class Program:

    def __init__(self):
        self.queues = {n: [] for n in ("sync", "gpsimd", "scalar", "tensor", "vector")}
        self.waited = {}

    def add(self, engine, issue, after=(), signal=None, inc=1):
        waits = []
        for event in after:
            if event is None:
                continue
            sig, value = event
            if self.waited.get((engine, sig), 0) < value:
                self.waited[engine, sig] = value
                waits.append((sig.handle, value))
        if signal is not None:
            signal.count += inc

        def run(eng):
            for handle, value in waits:
                eng.wait_ge(handle, value)
            ins = issue(eng)
            if signal is not None:
                ins.then_inc(signal.handle, inc)

        self.queues[engine].append(run)
        return None if signal is None else (signal, signal.count)


def build(nc, A, out):
    P = 128
    B, S, D = A["x"].shape
    KEYS = A["ctx_1024"].shape[1]
    TOKENS = B * S
    TILES = TOKENS // P
    E, _, F = A["L0_ffn_W1"].shape
    K = 2
    FC = F // P
    GT = 4
    GROUPS = TILES // GT
    EPS = 1e-5
    SCALE = float(D) ** -0.5
    CTX_TILES = B * KEYS // P
    REGION = TOKENS + P
    SLOT_TILES = K * TOKENS // P + E - 1
    TRASH = SLOT_TILES * P
    ROW = 2 * D + 2
    GUARD = 16.0
    assert GT * P == 2 * S and 2 * KEYS == P

    pr = Program()
    ctx = ExitStack()
    with ctx:
        def sb(name, shape, dt=F32):
            return ctx.enter_context(nc.sbuf_tensor(name, shape, dt))

        def signal(name):
            return Signal(ctx.enter_context(nc.semaphore(name)))

        bank = [ctx.enter_context(nc.psum_tensor(f"bank{i}", [P, 512], F32)) for i in range(8)]

        slots = nc.dram_tensor("slot_rows", (E * REGION + P, ROW), F16).ap()
        answers = nc.dram_tensor("answers", (TRASH + K * TOKENS, D), F32).ap()

        x_in = A["x"].rearrange("b s d -> (b s) d").rearrange("(i p) d -> p i d", p=P)
        out_v = out.rearrange("b s d -> (b s) d").rearrange("(i p) d -> p i d", p=P)
        ctx_in = A["ctx_1024"].rearrange("b s d -> (b s) d").rearrange("(i p) d -> p i d", p=P)
        ans_v = answers[TRASH:, :].rearrange("(i p) d -> p i d", p=P)

        ones = sb("ones", [P, P])
        ones16 = sb("ones16", [P, P], F16)
        ident = sb("ident", [P, P])
        ident16 = sb("ident16", [P, P], F16)
        mean_w = sb("mean_w", [P, P])
        below = sb("below", [P, P], BF16)
        onesb = sb("onesb", [P, P], BF16)
        iota_e = sb("iota_e", [P, GT, E])
        zero_rows = sb("zero_rows", [P, ROW], F16)
        trash_row = sb("trash_row", [P, SLOT_TILES])
        home_row = sb("home_row", [P, K, TILES], U32)
        tri = sb("tri", [1, E, E])
        slot_no = sb("slot_no", [1, SLOT_TILES])
        region0 = sb("region0", [P, E])

        x = sb("x_tok", [P, TILES, D])
        x2 = sb("x2", [P, TILES, D])
        cx = sb("cx", [P, CTX_TILES, D])
        cxT = sb("cxT", [P, CTX_TILES * P])
        w4 = sb("w4", [P, 4, D])
        woT = sb("woT", [P, D])
        wkq = sb("wkq", [P, D])
        wvo = sb("wvo", [P, D])
        bcol = sb("bcol", [P, 2])
        borow = sb("borow", [1, D])
        kb_col = sb("kb_col", [P, 1])
        vb_row = sb("vb_row", [1, D])
        kq = sb("kq", [P, CTX_TILES * P])
        kb_row = sb("kb_row", [1, CTX_TILES * P])
        vo = sb("vo", [P, CTX_TILES, D])
        wr = sb("wr", [P, E])
        brrow = sb("brrow", [1, E])

        w1f = sb("w1f", [P, E * F])
        w2f = sb("w2f", [P, E * FC, D])
        w1h = sb("w1h", [P, E * F], F16)
        w1l = sb("w1l", [P, E * F], F16)
        w2h = sb("w2h", [P, E * F], F16)
        w2l = sb("w2l", [P, E * F], F16)
        w2g = sb("w2g", [P, FC, D])
        w2c = sb("w2c", [P, FC, D])
        NB = E * F // P
        b1c = sb("b1c", [P, NB])
        b1h = sb("b1h", [P, NB], F16)
        b1l = sb("b1l", [P, NB], F16)
        b1t = sb("b1t", [P, E * F], F16)
        gb = sb("gb", [2 * NB, P])
        gbT = sb("gbT", [P, 2 * NB])
        g1s = sb("g1s", [P, NB])
        g1c, be1c = gbT[:, 0:NB], gbT[:, NB:2 * NB]
        b2row = sb("b2row", [1, E * D])
        c2row = sb("c2row", [1, E * D])
        c2 = sb("c2", [P, E * D])
        g2 = sb("g2", [P, E * D])
        be2 = sb("be2", [P, E * D])
        mx = sb("mx", [P, 4])
        mx4 = sb("mx4", [4, 1])
        dg4 = sb("dg4", [4, 4])
        mb = sb("mb", [P, 4])
        mm2 = sb("mm2", [P, 2])
        pw2 = sb("pw2", [P, 2], U32)
        sc = sb("sc", [P, 2])
        scg = sb("scg", [P, 2])
        sc2 = sb("sc2", [P, 2])
        epsS = sb("epsS", [P, 2])

        st1a = sb("st1a", [P, TILES, 6])
        mv1a = sb("mv1a", [P, TILES, 2])
        st = sb("st", [P, GT, 6])
        mv = sb("mv", [P, GT, 2])

        def root_work(name):
            return [sb(f"{name}{n}", [P, w])[:, :] for n, w in ((1, TILES), (2, GT))]

        ve, guess, y, yy, rstd = (root_work(n) for n in ("ve", "guess", "y", "yy", "rstd"))
        rstd1, rstd2 = rstd
        nmr1 = sb("nmr1", [P, TILES])
        nmr2 = sb("nmr2", [P, GT])
        xn = sb("xn", [P, GT, D])
        xnT = sb("xnT", [P, GT * P])
        smax = sb("smax", [P, 2, 2])
        nmax = sb("nmax", [P, 2, 2])
        prob = sb("prob", [P, 2, 2, KEYS])
        psum_ = sb("psum_", [P, 2, 2])
        rsum = sb("rsum", [P, 2, 2])
        pT = sb("pT", [P, 2, P])
        xt = sb("xt", [P, GT, D])
        xtT = sb("xtT", [P, GT * P])
        lg = sb("lg", [P, GT, E])
        top = sb("top", [P, TILES, 8])
        topi = sb("topi", [P, GT, 8], U32)
        oh = sb("oh", [P, K, GT, E])
        mask = sb("mask", [P, GT, E], BF16)
        filled = sb("filled", [P, 2, E])
        rank = sb("rank", [P, GT, E])
        pick = sb("pick", [P, K, GT, E])
        posf = sb("posf", [P, K, GT])
        pos = sb("pos", [P, 2, K, GT], U32)
        pay = [sb(f"pay{n}", [P, K, GT, ROW], F16) for n in range(2)]
        gd = sb("gd", [P, TILES])
        ge_ = sb("ge_", [P, TILES])
        gs = sb("gs", [P, TILES])
        gate = sb("gate", [P, K, TILES])

        cnt = sb("cnt", [1, E])
        cnti = sb("cnti", [1, E], I32)
        nti = sb("nti", [1, E], I32)
        ntf = sb("ntf", [1, E])
        ntri = sb("ntri", [1, E, E])
        cum = sb("cum", [1, E])
        full = sb("full", [1, SLOT_TILES, E])
        fulln = sb("fulln", [1, SLOT_TILES, E])
        sx = sb("sx", [1, SLOT_TILES])
        sfirst = sb("sfirst", [1, SLOT_TILES])
        sa = sb("sa", [1, SLOT_TILES])
        sb_ = sb("sb_", [1, SLOT_TILES])
        smin = sb("smin", [1, SLOT_TILES])
        row_tab = sb("row_tab", [1, SLOT_TILES], U32)
        off_w = sb("off_w", [1, SLOT_TILES], U32)
        off_d = sb("off_d", [1, SLOT_TILES], U32)
        tail = sb("tail", [1, E], U32)

        NX = 4
        NZ = 3
        xs = [sb(f"xs{n}", [P, ROW], F16) for n in range(NX)]
        xsT = [sb(f"xsT{n}", [P, 2 * P], F16) for n in range(2)]
        r = [sb(f"r{n}", [P, F]) for n in range(2)]
        rTh = [sb(f"rTh{n}", [P, F], F16) for n in range(2)]
        rTl = [sb(f"rTl{n}", [P, F], F16) for n in range(2)]
        st1 = [sb(f"st1_{n}", [P, 6]) for n in range(4)]
        mv1 = [sb(f"mv1_{n}", [P, 2]) for n in range(4)]
        sd1 = [sb(f"sd1_{n}", [P, 1]) for n in range(4)]
        rs1 = [sb(f"rs1_{n}", [P, 1]) for n in range(4)]
        u = [sb(f"u{n}", [P, D]) for n in range(3)]
        ur = [sb(f"ur{n}", [P, D]) for n in range(3)]
        st2 = [sb(f"st2_{n}", [P, 6]) for n in range(4)]
        mv2 = [sb(f"mv2_{n}", [P, 2]) for n in range(4)]
        sd2 = [sb(f"sd2_{n}", [P, 1]) for n in range(4)]
        rs2 = [sb(f"rs2_{n}", [P, 1]) for n in range(4)]
        z0 = [sb(f"z0_{n}", [P, D]) for n in range(2)]
        z1 = [sb(f"z1_{n}", [P, D]) for n in range(2)]
        z = [sb(f"z{n}", [P, D]) for n in range(NZ)]
        ND = 9
        dest = [sb(f"dest{n}", [P, 1], U32) for n in range(ND)]
        GD = GT * D

        def part_c(at, n):
            return w1f[:, at * GD:(at + n) * GD].rearrange("p (k i d) -> p k i d", k=n, i=GT)

        ya = [part_c(n * K, K) for n in range(2)]
        acc = [part_c(2 * K + n, 1)[:, 0, :, :] for n in range(2)]
        res = [part_c(2 * K + 2 + n, 1)[:, 0, :, :] for n in range(2)]

        def load(name, dst, src, engine="sync"):
            return pr.add(engine, lambda e: e.dma_start(dst, src), signal=signal("ld_" + name), inc=16)

        ev_cx = load("ctx", cx[:, :, :], ctx_in)
        ev_w4 = {n: load(n, w4[:, q, :], A[f"L0_xattn_{n}"], "scalar")
                 for q, n in enumerate(("Wk", "Wq", "Wv", "Wo"))}
        WK, WQ, WV, WO = (w4[:, q, :] for q in range(4))
        ev_bq = load("bq", bcol[:, 0:1], A["L0_xattn_bq"].rearrange("(p o) -> p o", o=1), "scalar")
        ev_bv = load("bv", bcol[:, 1:2], A["L0_xattn_bv"].rearrange("(p o) -> p o", o=1), "scalar")
        ev_bo = load("bo", borow[:, :], A["L0_xattn_bo"].rearrange("(o n) -> o n", o=1), "scalar")
        ev_x = [load(f"x{g}", x[:, g * GT:(g + 1) * GT, :], x_in[:, g * GT:(g + 1) * GT, :])
                for g in range(GROUPS)]
        ev_wr = load("wr", wr[:, :], A["L0_ffn_Wr"], "scalar")
        ev_br = load("br", brrow[:, :], A["L0_ffn_br"].rearrange("(o n) -> o n", o=1), "scalar")
        H = E // 2
        ev_w1 = [load(f"w1_{h}", w1f[:, h * H * F:(h + 1) * H * F].rearrange("p (e f) -> p e f", e=H),
                      A["L0_ffn_W1"][h * H:(h + 1) * H].rearrange("e d f -> d e f")) for h in range(2)]
        ev_w2 = [load(f"w2_{h}", w2f[:, h * H * FC:(h + 1) * H * FC, :],
                      A["L0_ffn_W2"][h * H:(h + 1) * H].rearrange("e (c p) d -> p (e c) d", p=P))
                 for h in range(2)]

        def flat(name):
            return A[name].rearrange("e f -> (e f)")

        ev_b1 = load("b1", b1c[:, :], flat("L0_ffn_b1").rearrange("(p c) -> p c", p=P))
        ev_gb = [load(n, gb[q * NB:(q + 1) * NB, :], flat("L0_ffn_" + n).rearrange("(c p) -> c p", p=P))
                 for q, n in enumerate(("g1", "be1"))]
        ev_b2 = load("b2", b2row[:, :], flat("L0_ffn_b2").rearrange("(o n) -> o n", o=1))
        ev_g2 = load("g2", g2[:, :], flat("L0_ffn_g2").rearrange("(o n) -> o n", o=1).to_broadcast([P, E * D]))
        ev_be2 = load("be2", be2[:, :], flat("L0_ffn_be2").rearrange("(o n) -> o n", o=1).to_broadcast([P, E * D]))

        s_const = signal("constants")

        def const(issue, after=()):
            return pr.add("gpsimd", issue, after, s_const)

        ev_ones = const(lambda e: e.memset(ones[:, :], 1.0))
        ev_ident = const(lambda e: e.affine_select(out=ident[:, :], in_=ones[:, :], compare_op=ALU.is_equal, fill=0.0,
                                        base=0, pattern=[[-1, P]], channel_multiplier=1), [ev_ones])
        const(lambda e: e.memset(ones16[:, :], 1.0))
        const(lambda e: e.memset(onesb[:, :], 1.0))
        const(lambda e: e.memset(mean_w[:, :], 1.0 / F))
        const(lambda e: e.memset(zero_rows[:, :], 0.0))
        const(lambda e: e.iota(iota_e[:, :, :], [[0, GT], [1, E]], base=0, channel_multiplier=0,
                               allow_small_or_imprecise_dtypes=True))
        const(lambda e: e.iota(trash_row[:, :], [[P, SLOT_TILES]], base=0, channel_multiplier=1,
                               allow_small_or_imprecise_dtypes=True))
        const(lambda e: e.iota(home_row[:, :, :], [[TOKENS, K], [P, TILES]], base=TRASH,
                               channel_multiplier=1))
        const(lambda e: e.iota(slot_no[:, :], [[1, SLOT_TILES]], base=0, channel_multiplier=0,
                               allow_small_or_imprecise_dtypes=True))
        for dst in (region0[:, :], filled[:, 0, :]):
            ev_iotas = const(lambda e, dst=dst: e.iota(dst, [[REGION, E]], base=0, channel_multiplier=0,
                                            allow_small_or_imprecise_dtypes=True))
        const(lambda e: e.affine_select(out=ident16[:, :], in_=ones16[:, :], compare_op=ALU.is_equal,
                                        fill=0.0, base=0, pattern=[[-1, P]], channel_multiplier=1), [ev_iotas])
        const(lambda e: e.affine_select(out=below[:, :], in_=onesb[:, :], compare_op=ALU.is_gt, fill=0.0,
                                        base=0, pattern=[[1, P]], channel_multiplier=-1))
        const(lambda e: e.affine_select(out=tri[:, :, :], in_=ones[0:1, 0:E * E].rearrange(
            "p (a b) -> p a b", a=E), compare_op=ALU.is_ge, fill=0.0, base=0, pattern=[[1, E], [-1, E]],
            channel_multiplier=0))
        ev_const = const(lambda e: e.memset(b1t[:, :].bitcast(U32), 0))

        s_pw, s_cw = signal("pe_attn_weights"), signal("copied_attn_weights")

        def pe(issue, after, sig):
            return pr.add("tensor", issue, after, sig)

        def mm(dst, lhsT, rhs, start=True, stop=True):
            return lambda e: e.matmul(dst, lhsT, rhs, start=start, stop=stop)

        def tp(dst, src, idn):
            return lambda e: e.transpose(dst, src, idn)

        b0, b1_, b2_, b3 = bank[0:4]
        pe(tp(b0[:, 0:D], WO, ident[:, :]), [ev_ident, ev_w4["Wo"]], s_pw)
        pe(mm(b0[:, D:2 * D], WK, WQ), [ev_w4["Wk"], ev_w4["Wq"]], s_pw)
        t = pe(mm(b0[:, 2 * D:2 * D + 1], WK, bcol[:, 0:1]), [ev_bq], s_pw)
        pr.add("vector", lambda e: e.tensor_copy(woT[:, :], b0[:, 0:D]), [t], s_cw)
        pr.add("vector", lambda e: e.tensor_copy(wkq[:, :], b0[:, D:2 * D]), [], s_cw)
        t = pr.add("vector", lambda e: e.tensor_copy(kb_col[:, :], b0[:, 2 * D:2 * D + 1]), [], s_cw)
        pe(mm(b1_[:, 0:D], WV, woT[:, :]), [t, ev_w4["Wv"]], s_pw)
        pe(mm(b1_[0:1, D:2 * D], bcol[:, 1:2], woT[:, :], stop=False), [ev_bv], s_pw)
        t = pe(mm(b1_[0:1, D:2 * D], ones[0:1, 0:1], borow[:, :], start=False), [ev_bo], s_pw)
        pr.add("vector", lambda e: e.tensor_copy(wvo[:, :], b1_[:, 0:D]), [t], s_cw)
        ev_wvo = pr.add("vector", lambda e: e.tensor_copy(vb_row[:, :], b1_[0:1, D:2 * D]), [], s_cw)
        s_ct, s_ctc = signal("pe_ctxT"), signal("copied_ctxT")
        halves = range(CTX_TILES * P // 512)
        ev_half = []
        for h in halves:
            for c in range(4):
                t = pe(tp(bank[2 + h][:, c * P:(c + 1) * P], cx[:, h * 4 + c, :], ident[:, :]), [ev_cx], s_ct)
            ev_half.append(pr.add("scalar", lambda e, h=h: e.activation(
                cxT[:, h * 512:(h + 1) * 512], bank[2 + h][:, :], ACT.Copy), [t], s_ctc))
        s_kq, s_kqc = signal("pe_keys"), signal("copied_keys")
        for h in halves:
            cols = slice(h * 512, (h + 1) * 512)
            t = pe(mm(bank[4 + h][:, :], wkq[:, :], cxT[:, cols]), [ev_half[h]], s_kq)
            pr.add("vector", lambda e, h=h, cols=cols: e.tensor_copy(kq[:, cols], bank[4 + h][:, :]),
                   [t], s_kqc)
            t = pe(mm(bank[6 + h][0:1, :], kb_col[:, :], cxT[:, cols]), [], s_kq)
            ev_kq = pr.add("vector", lambda e, h=h, cols=cols: e.tensor_copy(
                kb_row[:, cols], bank[6 + h][0:1, :]), [t], s_kqc)
        s_vo, s_voc = signal("pe_values"), signal("copied_values")
        for h in halves:
            for c in range(4):
                n = h * 4 + c
                pe(mm(bank[2 + h][:, c * P:(c + 1) * P], cxT[:, n * P:(n + 1) * P], wvo[:, :], stop=False),
                   [ev_wvo, ev_half[h]], s_vo)
                t = pe(mm(bank[2 + h][:, c * P:(c + 1) * P], ones[0:1, :], vb_row[:, :], start=False),
                       [], s_vo)
            ev_vo = pr.add("scalar", lambda e, h=h: e.activation(
                vo[:, h * 4:(h + 1) * 4, :], bank[2 + h][:, :].rearrange("p (c d) -> p c d", c=4), ACT.Copy),
                [t], s_voc)

        s = {n: signal(n) for n in (
            "stats", "guess", "newton", "nmr", "xn", "pe_xnT", "xnT", "pe_score", "smax", "prob", "rsum",
            "pe_pT", "pT", "pe_attn", "x2", "xt", "pe_xtT", "xtT", "pe_logit", "logit", "top", "pay_hi",
            "pay_lo", "pay_copy", "pe_rank", "rank", "pos", "scatter0", "scatter1")}
        done = {}
        plan = []

        def at(time, step, *args):
            plan.append((time, len(plan), step, args))

        def queue_plan():
            for _, _, step, args in sorted(plan, key=lambda p: p[:2]):
                step(*args)
            plan.clear()

        def vec(key, issue, after=()):
            return pr.add("vector", issue, after, s[key])

        def act(key, issue, after=()):
            return pr.add("scalar", issue, after, s[key])

        def inverse_root(n, var, after):
            v, g0, g1_, q = ve[n], guess[n], y[n], yy[n]
            t = vec("guess", lambda e: e.tensor_scalar(v, var, EPS, None, ALU.add), after)
            t = vec("guess", lambda e: e.tensor_scalar(g0.bitcast(U32), v.bitcast(U32), 1, None,
                                                       ALU.logical_shift_right), [t])
            t = vec("guess", lambda e: e.tensor_scalar(g1_.bitcast(U32), g0.bitcast(U32), -1.0,
                                                       float(0x5F3759DF), ALU.mult, ALU.add), [t])
            for k in range(3):
                dst = rstd[n] if k == 2 else g1_
                t = vec("newton", lambda e: e.tensor_tensor(q, g1_, g1_, ALU.mult), [t])
                t = vec("newton", lambda e: e.scalar_tensor_tensor(out=g0, in0=q, scalar=-0.5, in1=v,
                                                                   op0=ALU.mult, op1=ALU.mult), [t])
                t = vec("newton", lambda e, dst=dst: e.scalar_tensor_tensor(
                    out=dst, in0=g0, scalar=1.5, in1=g1_, op0=ALU.add, op1=ALU.mult), [t])
            return t

        def a_stats1(g):
            for i in range(GT):
                n = g * GT + i
                t = vec("stats", lambda e, n=n: e.bn_stats(st1a[:, n, :], x[:, n, :]), [ev_x[g]])
            for i in range(GT):
                n = g * GT + i
                t2 = vec("stats", lambda e, n=n: e.bn_aggr(mv1a[:, n, :], st1a[:, n, :]), [t])
            done["stats1"] = t2

        def a_rstd1():
            t = inverse_root(0, mv1a[:, :, 1], [done["stats1"]])
            done["nmr1"] = vec("nmr", lambda e: e.scalar_tensor_tensor(
                out=nmr1[:, :], in0=mv1a[:, :, 0], scalar=-1.0, in1=rstd[0], op0=ALU.mult, op1=ALU.mult), [t])

        def a_xn(g):
            for i in range(GT):
                n = g * GT + i
                done["xn", g] = act("xn", lambda e, i=i, n=n: e.activation(
                    xn[:, i, :], x[:, n, :], ACT.Identity, bias=nmr1[:, n:n + 1], scale=rstd1[:, n:n + 1]),
                    [done["nmr1"], done.get(("pe_xnT", g - 1))])

        def a_xnT(g):
            for i in range(GT):
                t = pe(tp(bank[0][:, i * P:(i + 1) * P], xn[:, i, :], ident[:, :]),
                       [done["xn", g], done.get(("xnT", g - 1))], s["pe_xnT"])
            done["pe_xnT", g] = t

        def a_xnT_copy(g):
            done["xnT", g] = act("xnT", lambda e: e.activation(xnT[:, :], bank[0][:, :], ACT.Copy),
                                 [done["pe_xnT", g], done.get(("pe_score", g - 1))])

        scores = bank[1][:, 0:4 * KEYS].rearrange("p (q b k) -> p q b k", q=2, b=2)

        def a_score(g):
            for i in range(GT):
                b, q = i // 2, i % 2
                keys = slice((2 * g + b) * KEYS, (2 * g + b + 1) * KEYS)
                dst = bank[1][:, (2 * q + b) * KEYS:(2 * q + b + 1) * KEYS]
                pe(mm(dst, xnT[:, i * P:(i + 1) * P], kq[:, keys], stop=False),
                   [done["xnT", g], ev_kq, done.get(("prob", g - 1))], s["pe_score"])
                t = pe(mm(dst, ones[0:1, :], kb_row[:, keys], start=False), [], s["pe_score"])
            done["pe_score", g] = t

        def a_max(g):
            t = vec("smax", lambda e: e.tensor_reduce(smax[:, :, :], scores, AX.X, ALU.max),
                    [done["pe_score", g]])
            done["smax", g] = vec("smax", lambda e: e.tensor_scalar(
                nmax[:, :, :], smax[:, :, :], -SCALE, None, ALU.mult), [t, done.get(("prob", g - 1))])

        def a_prob(g):
            for q in range(2):
                for b in range(2):
                    t = act("prob", lambda e, q=q, b=b: e.activation(
                        prob[:, q, b, :], scores[:, q, b, :], ACT.Exp, bias=nmax[:, q, b:b + 1], scale=SCALE,
                        accum_out=psum_[:, q, b:b + 1]),
                        [done["smax", g], done.get(("pe_pT", g - 1)), done.get(("rsum", g - 1))])
            done["prob", g] = t

        def a_rsum(g):
            done["rsum", g] = vec("rsum", lambda e: e.reciprocal(rsum[:, :, :], psum_[:, :, :]),
                                  [done["prob", g], done.get(("x2", g - 1))])

        def a_pT(g):
            for q in range(2):
                t = pe(tp(bank[2][:, q * P:(q + 1) * P],
                          prob[:, q, :, :].rearrange("p b k -> p (b k)"), ident[:, :]),
                       [done["prob", g], ev_vo, done.get(("pT", g - 1))], s["pe_pT"])
            done["pe_pT", g] = t

        def a_pT_copy(g):
            done["pT", g] = act("pT", lambda e: e.activation(
                pT[:, :, :], bank[2][:, 0:2 * P].rearrange("p (q k) -> p q k", q=2), ACT.Copy),
                [done["pe_pT", g], done.get(("pe_attn", g - 1))])

        def attn(b, q):
            return bank[3 + 4 * b][:, q * D:(q + 1) * D]

        def a_attend(g):
            for i in range(GT):
                b, q = i // 2, i % 2
                rows = slice(b * KEYS, (b + 1) * KEYS)
                t = pe(mm(attn(b, q), pT[rows, q, :], vo[rows, g, :]),
                       [done["pT", g], ev_kq, done.get(("x2", g - 1))], s["pe_attn"])
            done["pe_attn", g] = t

        def a_x2(g):
            for i in range(GT):
                b, q = i // 2, i % 2
                done["x2", g] = vec("x2", lambda e, i=i, b=b, q=q: e.scalar_tensor_tensor(
                    out=x2[:, g * GT + i, :], in0=attn(b, q), scalar=rsum[:, q, b:b + 1],
                    in1=x[:, g * GT + i, :], op0=ALU.mult, op1=ALU.add), [done["pe_attn", g], done["rsum", g]])

        def a_stats2(g):
            for i in range(GT):
                t = vec("stats", lambda e, i=i: e.bn_stats(st[:, i, :], x2[:, g * GT + i, :]), [done["x2", g]])
            for i in range(GT):
                t2 = vec("stats", lambda e, i=i: e.bn_aggr(mv[:, i, :], st[:, i, :]), [t])
            done["stats2", g] = t2

        def a_rstd2(g):
            t = inverse_root(1, mv[:, :, 1], [done["stats2", g], done.get(("xt", g - 1))])
            done["nmr2", g] = vec("nmr", lambda e: e.scalar_tensor_tensor(
                out=nmr2[:, :], in0=mv[:, :, 0], scalar=-1.0, in1=rstd[1], op0=ALU.mult, op1=ALU.mult), [t])

        def a_xt(g):
            for i in range(GT):
                done["xt", g] = act("xt", lambda e, i=i: e.activation(
                    xt[:, i, :], x2[:, g * GT + i, :], ACT.Identity, bias=nmr2[:, i:i + 1],
                    scale=rstd2[:, i:i + 1]),
                    [done["nmr2", g], done.get(("pe_xtT", g - 1)), done.get(("pay_lo", g - 1))])

        def a_xtT(g):
            for i in range(GT):
                t = pe(tp(bank[4][:, i * P:(i + 1) * P], xt[:, i, :], ident[:, :]),
                       [done["xt", g], done.get(("xtT", g - 1))], s["pe_xtT"])
            done["pe_xtT", g] = t

        def a_xtT_copy(g):
            done["xtT", g] = act("xtT", lambda e: e.activation(xtT[:, :], bank[4][:, :], ACT.Copy),
                                 [done["pe_xtT", g], done.get(("pe_logit", g - 1))])

        def a_logit(g):
            for i in range(GT):
                dst = bank[5][:, i * E:(i + 1) * E]
                pe(mm(dst, xtT[:, i * P:(i + 1) * P], wr[:, :], stop=False),
                   [done["xtT", g], ev_wr, ev_br, done.get(("rank", g - 1))], s["pe_logit"])
                t = pe(mm(dst, ones[0:1, :], brrow[:, :], start=False), [], s["pe_logit"])
            done["pe_logit", g] = t
            done["logit", g] = vec("logit", lambda e: e.tensor_copy(
                lg[:, :, :], bank[5][:, 0:GT * E].rearrange("p (i e) -> p i e", i=GT)), [t])

        def a_pay_hi(g):
            done["pay_hi", g] = act("pay_hi", lambda e: e.activation(
                pay[g % 2][:, 0, :, 0:D], xt[:, :, :], ACT.Copy), [done["xt", g], done.get(("scatter", g - 2))])

        def a_pay_lo(g):
            p = pay[g % 2]
            done["pay_lo", g] = t = vec("pay_lo", lambda e: e.tensor_tensor(
                p[:, 0, :, D:2 * D], xt[:, :, :], p[:, 0, :, 0:D], ALU.subtract), [done["pay_hi", g]])
            vec("pay_copy", lambda e: e.tensor_copy(
                p[:, :, :, 2 * D:2 * D + 2].bitcast(U32)[:, :, :, 0], home_row[:, :, g * GT:(g + 1) * GT]),
                [ev_const])
            done["pay", g] = vec("pay_copy", lambda e: e.tensor_copy(
                p[:, 1, :, 0:2 * D], p[:, 0, :, 0:2 * D]), [t])

        def a_top(g):
            for i in range(GT):
                t = vec("top", lambda e, i=i: e.max(top[:, g * GT + i, :], lg[:, i, :]), [done["logit", g]])
            for i in range(GT):
                t2 = vec("top", lambda e, i=i: e.max_index(topi[:, i, :], top[:, g * GT + i, :], lg[:, i, :]),
                         [t])
            for k in range(K):
                t = vec("top", lambda e, k=k: e.tensor_tensor(
                    oh[:, k, :, :], iota_e[:, :, :], topi[:, :, k:k + 1].to_broadcast([P, GT, E]),
                    ALU.is_equal), [t2, ev_const])
            done["mask", g] = vec("top", lambda e: e.tensor_tensor(
                mask[:, :, :], oh[:, 0, :, :], oh[:, 1, :, :], ALU.add), [t])

        def a_rank(g):
            m = mask[:, :, :].rearrange("p i e -> p (i e)")
            pe(mm(bank[5][:, 64:64 + GT * E], below[:, :], m, stop=False), [done["mask", g]], s["pe_rank"])
            for d in range(1, GT):
                pe(mm(bank[5][:, 64 + d * E:64 + GT * E], onesb[:, :], m[:, 0:(GT - d) * E], start=False,
                      stop=(d == GT - 1)), [], s["pe_rank"])
            for i in range(GT):
                t = pe(mm(bank[5][:, 128:128 + E], onesb[:, :], m[:, i * E:(i + 1) * E], start=(i == 0),
                          stop=(i == GT - 1)), [], s["pe_rank"])
            done["pe_rank", g] = t

        def a_pos(g):
            c, nx = g % 2, (g + 1) % 2
            vec("rank", lambda e: e.tensor_tensor(
                rank[:, :, :], bank[5][:, 64:64 + GT * E].rearrange("p (i e) -> p i e", i=GT),
                filled[:, c:c + 1, :].to_broadcast([P, GT, E]), ALU.add),
                [done["pe_rank", g], done.get(("rank", g - 1))])
            done["rank", g] = t = vec("rank", lambda e: e.tensor_tensor(
                filled[:, nx, :], bank[5][:, 128:128 + E], filled[:, c, :], ALU.add))
            for k in range(K):
                t2 = vec("pos", lambda e, k=k: e.tensor_tensor(pick[:, k, :, :], oh[:, k, :, :],
                                                               rank[:, :, :], ALU.mult), [t])
            t = vec("pos", lambda e: e.tensor_reduce(posf[:, :, :], pick[:, :, :, :], AX.X, ALU.add), [t2])
            done["pos", g] = vec("pos", lambda e: e.tensor_copy(pos[:, g % 2, :, :], posf[:, :, :]),
                                 [t, done.get(("scatter", g - 2))])

        def a_scatter(g, k, i):
            done["scatter", g] = pr.add("gpsimd", lambda e: e.indirect_dma_start(
                slots, bass.IndirectOffsetOnAxis(ap=pos[:, g % 2, k, i:i + 1], axis=0),
                pay[g % 2][:, k, i, :], None), [done["pos", g], done["pay", g]], s[f"scatter{g % 2}"], 16)

        s_scale, s_sp = signal("scale"), signal("pe_scale")

        def weight_scale():
            def top_abs(col, src, after):
                return pr.add("vector", lambda e: e.tensor_reduce(
                    mx[:, col:col + 1], src, AX.X, ALU.max, apply_absolute_value=True), after, s_scale)
            t = pe(tp(bank[6][:, 0:2 * NB], gb[:, :], ident[0:2 * NB, 0:2 * NB]), [*ev_gb, ev_kq], s_sp)
            ev_g1 = pr.add("vector", lambda e: e.tensor_copy(gbT[:, :], bank[6][:, 0:2 * NB]), [t], s_scale)
            top_abs(0, w1f[:, :], ev_w1)
            top_abs(1, b1c[:, :], [ev_b1])
            top_abs(2, w2f[:, :, :].rearrange("p c d -> p (c d)"), ev_w2)
            t = top_abs(3, g1c[:, :], [ev_g1])
            t = pe(tp(bank[6][0:4, 0:P], mx[:, :], ident[:, :]), [t, ev_kq], s_sp)

            def dv(issue, after):
                return pr.add("vector", issue, after, s_scale)
            t = dv(lambda e: e.tensor_reduce(mx4[:, :], bank[6][0:4, 0:P], AX.X, ALU.max), [t])
            t = dv(lambda e: e.tensor_scalar(dg4[:, :], ident[0:4, 0:4], mx4[:, 0:1], None, ALU.mult), [t])
            t = pe(mm(bank[6][:, 128:132], ones[0:4, :], dg4[:, :]), [t], s_sp)
            t = dv(lambda e: e.tensor_copy(mb[:, :], bank[6][:, 128:132]), [t])
            done["scale_bank"] = t
            dv(lambda e: e.tensor_tensor(mm2[:, 0:1], mb[:, 0:1], mb[:, 1:2], ALU.max), [t])
            t = dv(lambda e: e.scalar_tensor_tensor(out=mm2[:, 1:2], in0=mb[:, 2:3], scalar=2.0,
                                                    in1=mb[:, 3:4], op0=ALU.mult, op1=ALU.mult), [])
            t = dv(lambda e: e.tensor_scalar(mb[:, 0:2], mm2[:, :], 1e-30, 1e30, ALU.max, ALU.min), [t])
            t = dv(lambda e: e.tensor_scalar(pw2[:, :], mb[:, 0:2].bitcast(U32), 0x7F800000, None,
                                             ALU.bitwise_and), [t])
            t = dv(lambda e: e.reciprocal(scg[:, :], pw2[:, :].bitcast(F32)), [t])
            t = dv(lambda e: e.tensor_scalar(sc[:, :], scg[:, :], GUARD, None, ALU.mult), [t])
            t = dv(lambda e: e.tensor_tensor(sc2[:, :], sc[:, :], sc[:, :], ALU.mult), [t])
            dv(lambda e: e.tensor_scalar(g1s[:, :], g1c, sc[:, 1:2], None, ALU.mult), [])
            done["scale"] = dv(lambda e: e.tensor_scalar(epsS[:, :], sc2[:, :], EPS, None, ALU.mult), [t])
            t = dv(lambda e: e.tensor_scalar(b1h[:, :], b1c[:, :], sc[:, 0:1], None, ALU.mult),
                   [done["scale"]])
            t = dv(lambda e: e.scalar_tensor_tensor(out=b1l[:, :], in0=b1c[:, :], scalar=sc[:, 0:1],
                                                    in1=b1h[:, :], op0=ALU.mult, op1=ALU.subtract), [t])
            s_b1 = signal("b1_rows")
            for n, src in enumerate((b1h, b1l)):
                done["b1t"] = pr.add("sync", lambda e, n=n, src=src: e.dma_start(
                    b1t[n:n + 1, :].rearrange("o (p c) -> o p c", p=P), src[:, :]), [t, ev_const], s_b1, 16)

        s_w = {n: signal(n) for n in ("w_hi", "w_lo", "w2g", "w2c", "pe_w2", "c2row", "pe_c2", "c2")}

        def cols(t, e_):
            return t[:, e_ * F:(e_ + 1) * F]

        def chunks(t, e_):
            return cols(t, e_).rearrange("p (c d) -> p c d", c=FC)

        def w_up(e_):
            t = pr.add("scalar", lambda e: e.activation(cols(w1h, e_), cols(w1f, e_), ACT.Copy,
                                                        scale=sc[:, 0:1]), [done["scale"]], s_w["w_hi"])
            done["w1h", e_] = t

        def w_up_lo(e_):
            pr.add("vector", lambda e: e.scalar_tensor_tensor(
                out=cols(w1l, e_), in0=cols(w1f, e_), scalar=sc[:, 0:1], in1=cols(w1h, e_), op0=ALU.mult,
                op1=ALU.subtract), [done["w1h", e_]], s_w["w_lo"])

        def w_gained(e_):
            for c in range(FC):
                n = e_ * FC + c
                done["w2g", e_] = pr.add("scalar", lambda e, n=n, c=c: e.activation(
                    w2g[:, c, :], w2f[:, n, :], ACT.Copy, scale=g1s[:, n:n + 1]),
                    [done["scale"], done.get(("w2c", e_ - 1))], s_w["w2g"])

        def w_mean(e_):
            for c in range(FC):
                t = pe(mm(bank[6][:, 0:D], mean_w[:, :], w2g[:, c, :], start=(c == 0), stop=(c == FC - 1)),
                       [done["w2g", e_], done.get(("c2row", e_ - 1))], s_w["pe_w2"])
            done["w_mean", e_] = t

        def w_centred(e_):
            done["w2c", e_] = pr.add("vector", lambda e: e.tensor_tensor(
                w2c[:, :, :], w2g[:, :, :],
                bank[6][:, 0:D].rearrange("p (c d) -> p c d", c=1).to_broadcast([P, FC, D]), ALU.subtract),
                [done["w_mean", e_], done.get(("w_lo2", e_ - 1))], s_w["w2c"])

        def w_offset(e_):
            for c in range(FC):
                n = e_ * FC + c
                pe(mm(bank[6][0:1, 128:128 + D], be1c[:, n:n + 1], w2f[:, n, :], start=(c == 0), stop=False),
                   [done["w2c", e_]], s_w["pe_w2"])
            done["pe_w2", e_] = pe(mm(bank[6][0:1, 128:128 + D], ones[0:1, 0:1],
                                      b2row[:, e_ * D:(e_ + 1) * D], start=False), [ev_b2], s_w["pe_w2"])

        def w_offset_copy(e_):
            done["c2row", e_] = pr.add("vector", lambda e: e.tensor_scalar(
                c2row[:, e_ * D:(e_ + 1) * D], bank[6][0:1, 128:128 + D], sc[0:1, 1:2], None, ALU.mult),
                [done["pe_w2", e_]], s_w["c2row"])

        def w_down(e_):
            done["w2h", e_] = pr.add("scalar", lambda e: e.activation(
                chunks(w2h, e_), w2c[:, :, :], ACT.Copy), [done["w2c", e_]], s_w["w_hi"])

        def w_down_lo(e_):
            done["w_lo2", e_] = pr.add("vector", lambda e: e.tensor_tensor(
                chunks(w2l, e_), w2c[:, :, :], chunks(w2h, e_), ALU.subtract), [done["w2h", e_]],
                s_w["w_lo"])

        def w_spread():
            for h in range(E * D // 512):
                hc = slice(h * 512, (h + 1) * 512)
                t = pe(mm(bank[6][:, :], ones[0:1, :], c2row[:, hc]), [done["c2row", E - 1], done.get("c2")],
                       s_w["pe_c2"])
                done["c2"] = pr.add("scalar", lambda e, hc=hc: e.activation(
                    c2[:, hc], bank[6][:, :], ACT.Copy), [t], s_w["c2"])

        T = 8.5
        for g in range(GROUPS):
            at(3.4 + 1.1 * g, a_stats1, g)
        at(12.5, a_rstd1)
        A0 = 14.0
        for g in range(GROUPS):
            for time, step in ((0.0, a_xn), (1.2, a_xnT), (1.9, a_xnT_copy), (2.6, a_score), (3.8, a_max),
                               (4.6, a_prob), (5.5, a_rsum), (5.5, a_pT), (6.0, a_pT_copy), (6.5, a_attend),
                               (7.7, a_x2), (8.8, a_stats2), (10.0, a_rstd2), (11.4, a_xt), (12.4, a_xtT),
                               (13.0, a_xtT_copy), (13.8, a_logit), (13.7, a_pay_hi), (14.6, a_top),
                               (15.8, a_pay_lo), (15.8, a_rank), (16.6, a_pos)):
                at(A0 + T * g + time, step, g)
            for n in range(K * GT):
                at(A0 + T * g + 18 + n, a_scatter, g, n // GT, n % GT)
        at(A0 + 10.2, weight_scale)
        for e_ in range(E):
            for time, step in ((0.0, w_up), (0.9, w_up_lo), (0.9, w_gained), (2.0, w_mean), (3.2, w_centred),
                               (4.2, w_offset), (4.2, w_down), (5.2, w_offset_copy), (5.4, w_down_lo)):
                at(A0 + 22 + 7.0 * e_ + time, step, e_)
        at(A0 + 22 + 7.0 * E, w_spread)
        queue_plan()

        s_tab = signal("tables")

        def tab(issue, after=()):
            return pr.add("vector", issue, after, s_tab)

        fin = GROUPS % 2
        last = done["rank", GROUPS - 1]
        ev_tail = tab(lambda e: e.tensor_copy(tail[:, :], filled[0:1, fin, :]), [last])
        t = tab(lambda e: e.tensor_tensor(cnt[:, :], filled[0:1, fin, :], region0[0:1, :], ALU.subtract))
        t = tab(lambda e: e.tensor_scalar(cnti[:, :], cnt[:, :], float(P - 1), None, ALU.add), [t])
        t = tab(lambda e: e.tensor_scalar(nti[:, :], cnti[:, :], P.bit_length() - 1, None,
                                          ALU.arith_shift_right), [t])
        t = tab(lambda e: e.tensor_copy(ntf[:, :], nti[:, :]), [t])
        as_row = lambda ap, n: ap.rearrange("p (a e) -> p a e", a=1).to_broadcast([1, n, E])
        t = tab(lambda e: e.tensor_tensor(ntri[:, :, :], tri[:, :, :], as_row(ntf[:, :], E), ALU.mult), [t])
        t = tab(lambda e: e.tensor_reduce(cum[:, :], ntri[:, :, :], AX.X, ALU.add), [t])
        t = tab(lambda e: e.tensor_tensor(
            full[:, :, :], as_row(cum[:, :], SLOT_TILES),
            slot_no[:, :].rearrange("p (j a) -> p j a", a=1).to_broadcast([1, SLOT_TILES, E]), ALU.is_le), [t])
        tab(lambda e: e.tensor_reduce(sx[:, :], full[:, :, :], AX.X, ALU.add), [t])
        t = tab(lambda e: e.tensor_tensor(fulln[:, :, :], full[:, :, :], as_row(ntf[:, :], SLOT_TILES),
                                          ALU.mult))
        t = tab(lambda e: e.tensor_reduce(sfirst[:, :], fulln[:, :, :], AX.X, ALU.add), [t])
        t = tab(lambda e: e.tensor_tensor(sa[:, :], slot_no[:, :], sfirst[:, :], ALU.subtract), [t])
        t = tab(lambda e: e.tensor_scalar(sb_[:, :], sx[:, :], float(REGION), None, ALU.mult), [t])
        t = tab(lambda e: e.scalar_tensor_tensor(out=sa[:, :], in0=sa[:, :], scalar=float(P), in1=sb_[:, :],
                                                 op0=ALU.mult, op1=ALU.add), [t])
        tab(lambda e: e.tensor_scalar(row_tab[:, :], sa[:, :], float(E * REGION), None, ALU.min), [t])
        t = tab(lambda e: e.tensor_scalar(smin[:, :], sx[:, :], float(E - 1), None, ALU.min))
        tab(lambda e: e.tensor_scalar(off_w[:, :], smin[:, :], float(F), None, ALU.mult), [t])
        ev_tab = tab(lambda e: e.tensor_scalar(off_d[:, :], smin[:, :], float(D), None, ALU.mult), [t])

        s_zero = signal("zeroed")

        def zero_tail(e_):
            def issue(eng):
                row = eng.value_load(tail[0:1, e_:e_ + 1], min_val=e_ * REGION, max_val=e_ * REGION + TOKENS)
                return eng.dma_start(slots[bass.ds(row, P), :], zero_rows[:, :])
            return issue

        for e_ in range(E):
            pr.add("sync", zero_tail(e_), [ev_tail, ev_const], s_zero, 16)
        ev_zero = pr.add("sync", lambda e: e.dma_start(slots[E * REGION:, :], zero_rows[:, :]), [], s_zero, 16)

        s.update({n: signal(n) for n in (
            "pe_xsT", "xsT", "pe_h", "relu1", "bstats1", "std1", "rstd1", "pe_rT", "rT_hi", "rT_lo", "pe_y",
            "affine", "relu2", "bstats2", "std2", "rstd2", "z0", "z", "dest")})
        s_rows = [signal(f"rows{n}") for n in range(NX)]
        s_ans = [signal(f"answer{n}") for n in range(NZ)]
        scattered = [done["scatter", GROUPS - 1], done["scatter", GROUPS - 2]]
        psX, psH, psT, psY = bank[0:2], bank[2:4], bank[4:6], bank[6:8]
        W_MAX, D_MAX = (E - 1) * F, (E - 1) * D
        regs = {}

        def b_load(j):
            def issue(eng):
                row = eng.value_load(row_tab[0:1, j:j + 1], min_val=0, max_val=E * REGION)
                return eng.dma_start(xs[j % NX][:, :], slots[bass.ds(row, P), :])
            done["rows", j] = pr.add("sync", issue, [ev_tab, ev_zero, *scattered,
                                                     done.get(("pe_xsT", j - NX)), done.get(("dest", j - NX))],
                                     s_rows[j % NX], 16)

        def turned(j):
            return psX[j % 2][:, 0:P].bitcast(F16)

        def b_turn(j):
            for n in range(2):
                t = pe(tp(turned(j)[:, n * P:(n + 1) * P], xs[j % NX][:, n * D:(n + 1) * D], ident16[:, :]),
                       [done["rows", j], done.get(("xsT", j - 2)), done.get("phase")], s["pe_xsT"])
            done["pe_xsT", j] = t

        def b_turn_copy(j):
            done["xsT", j] = act("xsT", lambda e: e.activation(xsT[j % 2][:, :], turned(j), ACT.Copy),
                                 [done["pe_xsT", j], done.get(("pe_h", j - 2))])

        def b_dest(j):
            done["dest", j] = vec("dest", lambda e: e.tensor_tensor(
                dest[j % ND][:, :], xs[j % NX][:, 2 * D:2 * D + 2].bitcast(U32), trash_row[:, j:j + 1],
                ALU.max), [done["rows", j], done.get(("answer", j - ND))])

        def b_up(j):
            hi, lo = xsT[j % 2][:, 0:P], xsT[j % 2][:, P:2 * P]
            dst = psH[j % 2][:, :]

            def issue(eng):
                off = regs["pe", j] = eng.value_load(off_w[0:1, j:j + 1], min_val=0, max_val=W_MAX)
                w = lambda t: t[:, bass.ds(off, F)]
                eng.matmul(dst, ones16[:, :], w(b1t), start=True, stop=False)
                eng.matmul(dst, hi, w(w1h), start=False, stop=False)
                eng.matmul(dst, hi, w(w1l), start=False, stop=False)
                return eng.matmul(dst, lo, w(w1h), start=False, stop=True)
            done["pe_h", j] = pe(issue, [done["xsT", j], done.get(("relu1", j - 2)), done["b1t"],
                                         done["w_lo2", E - 1], ev_tab], s["pe_h"])

        def b_relu(j):
            done["relu1", j] = act("relu1", lambda e: e.activation(r[j % 2][:, :], psH[j % 2][:, :], ACT.Relu),
                                   [done["pe_h", j], done.get(("pe_rT", j - 2)), done.get(("bstats1", j - 2))])

        def b_stats(j):
            done["bstats1", j] = vec("bstats1", lambda e: e.bn_stats(st1[j % 4][:, :], r[j % 2][:, :]),
                                     [done["relu1", j]])

        def b_aggr(j):
            done["aggr1", j] = vec("bstats1", lambda e: e.bn_aggr(mv1[j % 4][:, :], st1[j % 4][:, :]),
                                   [done["bstats1", j]])

        def b_std(j):
            done["std1", j] = act("std1", lambda e: e.activation(
                sd1[j % 4][:, :], mv1[j % 4][:, 1:2], ACT.Sqrt, bias=epsS[:, 0:1]), [done["aggr1", j]])

        def b_rstd(j):
            done["rstd1", j] = vec("rstd1", lambda e: e.reciprocal(rs1[j % 4][:, :], sd1[j % 4][:, :]),
                                   [done["std1", j]])

        def b_turn_r(j):
            for c in range(FC):
                t = pe(tp(psT[j % 2][:, c * P:(c + 1) * P], r[j % 2][:, c * P:(c + 1) * P], ident[:, :]),
                       [done["relu1", j], done.get(("rT_lo", j - 2))], s["pe_rT"])
            done["pe_rT", j] = t

        def b_rT_hi(j):
            done["rT_hi", j] = act("rT_hi", lambda e: e.activation(rTh[j % 2][:, :], psT[j % 2][:, :], ACT.Copy),
                                   [done["pe_rT", j], done.get(("pe_y", j - 2))])

        def b_rT_lo(j):
            done["rT_lo", j] = vec("rT_lo", lambda e: e.tensor_tensor(
                rTl[j % 2][:, :], psT[j % 2][:, :], rTh[j % 2][:, :], ALU.subtract), [done["rT_hi", j]])

        def b_down(j):
            dst = psY[j % 2][:, 0:D]

            def issue(eng):
                off = regs["pe", j]
                for c in range(FC):
                    hi, lo = (t[j % 2][:, c * P:(c + 1) * P] for t in (rTh, rTl))
                    wh, wl = (t[:, bass.ds(off + c * D, D)] for t in (w2h, w2l))
                    eng.matmul(dst, hi, wh, start=(c == 0), stop=False)
                    eng.matmul(dst, hi, wl, start=False, stop=False)
                    ins = eng.matmul(dst, lo, wh, start=False, stop=(c == FC - 1))
                return ins
            done["pe_y", j] = pe(issue, [done["rT_lo", j], done.get(("affine", j - 2))], s["pe_y"])

        def b_affine(j):
            def issue(eng):
                off = eng.value_load(off_d[0:1, j:j + 1], min_val=0, max_val=D_MAX)
                return eng.scalar_tensor_tensor(out=u[j % 3][:, :], in0=psY[j % 2][:, 0:D],
                                                scalar=rs1[j % 4][:, 0:1], in1=c2[:, bass.ds(off, D)],
                                                op0=ALU.mult, op1=ALU.add)
            done["affine", j] = vec("affine", issue, [done["pe_y", j], done["rstd1", j], done["c2"],
                                                      done.get(("relu2", j - 3))])

        def b_relu2(j):
            done["relu2", j] = act("relu2", lambda e: e.activation(ur[j % 3][:, :], u[j % 3][:, :], ACT.Relu),
                                   [done["affine", j], done.get(("z0", j - 3))])

        def b_stats2(j):
            done["bstats2", j] = vec("bstats2", lambda e: e.bn_stats(st2[j % 4][:, :], ur[j % 3][:, :]),
                                     [done["relu2", j]])

        def b_aggr2(j):
            done["aggr2", j] = vec("bstats2", lambda e: e.bn_aggr(mv2[j % 4][:, :], st2[j % 4][:, :]),
                                   [done["bstats2", j]])

        def b_std2(j):
            done["std2", j] = act("std2", lambda e: e.activation(
                sd2[j % 4][:, :], mv2[j % 4][:, 1:2], ACT.Sqrt, bias=epsS[:, 1:2]), [done["aggr2", j]])

        def b_rstd2(j):
            done["rstd2", j] = vec("rstd2", lambda e: e.reciprocal(rs2[j % 4][:, :], sd2[j % 4][:, :]),
                                   [done["std2", j]])

        def b_norm(j):
            done["z0", j] = vec("z0", lambda e: e.tensor_scalar(
                z0[j % 2][:, :], ur[j % 3][:, :], mv2[j % 4][:, 0:1], rs2[j % 4][:, 0:1], ALU.subtract,
                ALU.mult), [done["rstd2", j], done.get(("z1", j - 2))])

        def b_out(j):
            pool = lambda issue, after=(): pr.add("gpsimd", issue, after, s["z"])

            def scaled(eng):
                off = regs["pool", j] = eng.value_load(off_d[0:1, j:j + 1], min_val=0, max_val=D_MAX)
                return eng.tensor_tensor(z1[j % 2][:, :], z0[j % 2][:, :], g2[:, bass.ds(off, D)], ALU.mult)
            t = done["z1", j] = pool(scaled, [done["z0", j], ev_g2, ev_be2, ev_tab])
            done["z", j] = pool(lambda e: e.tensor_tensor(
                z[j % NZ][:, :], z1[j % 2][:, :], be2[:, bass.ds(regs["pool", j], D)], ALU.add),
                [t, done.get(("answer", j - NZ))])

        def b_answer(j):
            done["answer", j] = pr.add("gpsimd", lambda e: e.indirect_dma_start(
                answers, bass.IndirectOffsetOnAxis(ap=dest[j % ND][:, 0:1], axis=0), z[j % NZ][:, :], None),
                [done["z", j], done["dest", j]], s_ans[j % NZ], 16)

        s_g = signal("gates")
        t = pr.add("vector", lambda e: e.tensor_tensor(gd[:, :], top[:, :, 1], top[:, :, 0], ALU.subtract),
                   [last], s_g)
        s_ge = signal("gate_exp")
        t = pr.add("scalar", lambda e: e.activation(ge_[:, :], gd[:, :], ACT.Exp), [t], s_ge)
        t = pr.add("vector", lambda e: e.tensor_scalar(gs[:, :], ge_[:, :], 1.0, None, ALU.add), [t], s_g)
        t = pr.add("vector", lambda e: e.reciprocal(gate[:, 0, :], gs[:, :]), [t], s_g)
        ev_gate = pr.add("vector", lambda e: e.tensor_tensor(gate[:, 1, :], ge_[:, :], gate[:, 0, :],
                                                             ALU.mult), [t], s_g)
        done["phase"] = ev_gate

        T = 2.25
        for j in range(SLOT_TILES):
            for time, step in ((0.5 - NX * T, b_load), (0.0, b_turn), (0.4, b_turn_copy), (0.4, b_dest),
                               (0.9, b_up), (2.0, b_relu), (2.75, b_turn_r), (2.75, b_stats), (3.6, b_aggr),
                               (3.45, b_rT_hi), (4.1, b_rT_lo), (3.95, b_std), (4.75, b_rstd), (4.95, b_down),
                               (5.8, b_affine), (6.3, b_relu2), (6.8, b_stats2), (7.2, b_aggr2),
                               (7.5, b_std2), (7.9, b_rstd2), (8.1, b_norm), (8.5, b_out), (9.5, b_answer)):
                at(j * T + time, step, j)
        queue_plan()

        s_ya = [signal(f"back{n}") for n in range(2)]
        s_c = signal("combined")
        s_out = [signal(f"stored{n}") for n in range(2)]
        answered = [done["answer", SLOT_TILES - 1 - n] for n in range(NZ)]
        for g in range(GROUPS):
            tiles = slice(g * GT, (g + 1) * GT)
            for k in range(K):
                t = pr.add("sync", lambda e, k=k, g=g: e.dma_start(
                    ya[g % 2][:, k, :, :], ans_v[:, k * TILES + g * GT:k * TILES + (g + 1) * GT, :]),
                    [*answered, done.get(("comb", g - 2))], s_ya[g % 2], 16)
            for i in range(GT):
                n = g * GT + i
                t1 = pr.add("vector", lambda e, g=g, i=i, n=n: e.scalar_tensor_tensor(
                    out=acc[g % 2][:, i, :], in0=ya[g % 2][:, 0, i, :], scalar=gate[:, 0, n:n + 1],
                    in1=x2[:, n, :], op0=ALU.mult, op1=ALU.add), [t, ev_gate], s_c)
            for i in range(GT):
                n = g * GT + i
                t2 = pr.add("vector", lambda e, g=g, i=i, n=n: e.scalar_tensor_tensor(
                    out=res[g % 2][:, i, :], in0=ya[g % 2][:, 1, i, :], scalar=gate[:, 1, n:n + 1],
                    in1=acc[g % 2][:, i, :], op0=ALU.mult, op1=ALU.add), [t1, done.get(("out", g - 2))], s_c)
            done["comb", g] = t2
            done["out", g] = pr.add("scalar", lambda e, g=g, tiles=tiles: e.dma_start(
                out_v[:, tiles, :], res[g % 2][:, :, :]), [t2], s_out[g % 2], 16)

        final = [done["out", GROUPS - 1], done["out", GROUPS - 2], ev_zero, *scattered, *answered]

        block = ctx.enter_context(nc.Block())
        for name in ("sync", "gpsimd", "scalar", "tensor", "vector"):
            def body(eng, name=name):
                for run in pr.queues[name]:
                    run(eng)
                if name == "sync":
                    for sig, value in final:
                        eng.wait_ge(sig.handle, value)
            {"sync": block.sync, "gpsimd": block.gpsimd, "scalar": block.scalar, "tensor": block.tensor,
             "vector": block.vector}[name](body)


_INS = ["x", "ctx_1024", "L0_xattn_Wk", "L0_xattn_Wv", "L0_xattn_bv", "L0_xattn_Wq", "L0_xattn_bq",
        "L0_xattn_Wo", "L0_xattn_bo", "L0_ffn_Wr", "L0_ffn_br", "L0_ffn_W1", "L0_ffn_b1", "L0_ffn_g1",
        "L0_ffn_be1", "L0_ffn_W2", "L0_ffn_b2", "L0_ffn_g2", "L0_ffn_be2"]


def kernel(**inputs):
    import concourse.bacc as bacc
    from concourse.bass_utils import run_bass_kernel_spmd

    nc = bacc.Bacc("TRN2", target_bir_lowering=False, num_devices=1)
    arrays, args = {}, {}
    for name in _INS:
        a = np.ascontiguousarray(inputs[name])
        arrays[f"in_{name}"] = a
        args[name] = nc.dram_tensor(f"in_{name}", a.shape, mybir.dt.from_np(a.dtype),
                                    kind="ExternalInput").ap()
    out = nc.dram_tensor("out_0", inputs["x"].shape, mybir.dt.float32, kind="ExternalOutput").ap()
    build(nc, args, out)
    r = run_bass_kernel_spmd(nc, [arrays], core_ids=[0])
    return r.results[0]["out_0"]
```

```python
import concourse.bass as bass
import numpy as np
from concourse import mybir
from contextlib import ExitStack

F32, F16, BF16, U32, I32 = (mybir.dt.float32, mybir.dt.float16, mybir.dt.bfloat16, mybir.dt.uint32,
                            mybir.dt.int32)
ALU = mybir.AluOpType
ACT = mybir.ActivationFunctionType
AX = mybir.AxisListType


class Signal:

    def __init__(self, handle):
        self.handle, self.count = handle, 0


class Program:

    def __init__(self):
        self.queues = {n: [] for n in ("sync", "gpsimd", "scalar", "tensor", "vector")}
        self.waited = {}

    def add(self, engine, issue, after=(), signal=None, inc=1):
        waits = []
        for event in after:
            if event is None:
                continue
            sig, value = event
            if self.waited.get((engine, sig), 0) < value:
                self.waited[engine, sig] = value
                waits.append((sig.handle, value))
        if signal is not None:
            signal.count += inc

        def run(eng):
            for handle, value in waits:
                eng.wait_ge(handle, value)
            ins = issue(eng)
            if signal is not None:
                ins.then_inc(signal.handle, inc)

        self.queues[engine].append(run)
        return None if signal is None else (signal, signal.count)


def build(nc, A, out):
    P = 128
    B, S, D = A["x"].shape
    KEYS = A["ctx_1024"].shape[1]
    TOKENS = B * S
    TILES = TOKENS // P
    E, _, F = A["L0_ffn_W1"].shape
    K = 2
    FC = F // P
    GT = 4
    GROUPS = TILES // GT
    EPS = 1e-5
    SCALE = float(D) ** -0.5
    CTX_TILES = B * KEYS // P
    REGION = TOKENS + P
    SLOT_TILES = K * TOKENS // P + E - 1
    TRASH = SLOT_TILES * P
    PACK = 7
    PACKS = -(-SLOT_TILES // PACK)
    BITS = (E - 1).bit_length()
    ROW = 2 * D + 2
    MANTISSA, BIAS = 23, 127
    SC_TOP = (74, 77)
    PACE = 0.2
    assert GT * P == 2 * S and 2 * KEYS == P

    pr = Program()
    ctx = ExitStack()
    with ctx:
        def sb(name, shape, dt=F32):
            return ctx.enter_context(nc.sbuf_tensor(name, shape, dt))

        def signal(name):
            return Signal(ctx.enter_context(nc.semaphore(name)))

        bank = [ctx.enter_context(nc.psum_tensor(f"bank{i}", [P, 512], F32)) for i in range(8)]

        slots = nc.dram_tensor("slot_rows", (E * REGION + P, ROW), F16).ap()
        answers = nc.dram_tensor("answers", (TRASH + K * TOKENS, D), F32).ap()

        x_in = A["x"].rearrange("b s d -> (b s) d").rearrange("(i p) d -> p i d", p=P)
        out_v = out.rearrange("b s d -> (b s) d").rearrange("(i p) d -> p i d", p=P)
        ctx_in = A["ctx_1024"].rearrange("b s d -> (b s) d").rearrange("(i p) d -> p i d", p=P)
        ans_v = answers[TRASH:, :].rearrange("(i p) d -> p i d", p=P)

        ones = sb("ones", [P, P])
        ones16 = sb("ones16", [P, P], F16)
        ident = sb("ident", [P, P])
        ident16 = sb("ident16", [P, P], F16)
        pick_row = sb("pick_row", [2, 2, P])
        second = sb("second", [1, 2])
        below = sb("below", [P, P], BF16)
        onesb = sb("onesb", [P, P], BF16)
        iota_e = sb("iota_e", [P, GT, E])
        zero_rows = sb("zero_rows", [P, ROW], F16)
        trash_row = sb("trash_row", [P, SLOT_TILES])
        home_row = sb("home_row", [P, K, TILES], U32)
        tri = sb("tri", [1, E, E])
        slot_no = sb("slot_no", [1, PACKS * PACK])
        region0 = sb("region0", [P, E])

        x = sb("x_tok", [P, TILES, D])
        x2 = sb("x2", [P, TILES, D])
        cx = sb("cx", [P, CTX_TILES, D])
        cxT = sb("cxT", [P, CTX_TILES * P])
        w4 = sb("w4", [P, 4, D])
        woT = sb("woT", [P, D])
        wkq = sb("wkq", [P, D])
        wvo = sb("wvo", [P, D])
        bcol = sb("bcol", [P, 2])
        borow = sb("borow", [1, D])
        kb_col = sb("kb_col", [P, 1])
        vb_row = sb("vb_row", [1, D])
        kq = sb("kq", [P, CTX_TILES * P])
        kb_row = sb("kb_row", [1, CTX_TILES * P])
        vo = sb("vo", [P, CTX_TILES, D])
        wr = sb("wr", [P, E])
        brrow = sb("brrow", [1, E])

        w1f = sb("w1f", [P, E * F])
        w2f = sb("w2f", [P, E * FC, D])
        w1h = sb("w1h", [P, E * F], F16)
        w1l = sb("w1l", [P, E * F], F16)
        w2h = sb("w2h", [P, E * F], F16)
        w2l = sb("w2l", [P, E * F], F16)
        w2_mean = sb("w2_mean", [P, E * D])
        w2g = sb("w2g", [P, FC, D])
        w2c = sb("w2c", [P, FC, D])
        NB = E * F // P
        b1c = sb("b1c", [P, NB])
        b1h = sb("b1h", [P, NB], F16)
        b1l = sb("b1l", [P, NB], F16)
        b1t = sb("b1t", [P, E * F], F16)
        gb = sb("gb", [2 * NB, P])
        gbT = sb("gbT", [P, 2 * NB])
        gm = sb("gm", [P, NB, 2])
        g1c = gbT[:, 0:NB]
        b2row = sb("b2row", [1, E * D])
        w2_rows = sb("w2_rows", [2, E * D])
        c2 = sb("c2", [P, E * D])
        g2 = sb("g2", [P, E * D])
        be2 = sb("be2", [P, E * D])
        ss = sb("ss", [P, 4])
        gmax = sb("gmax", [P, 1])
        total = sb("total", [P, 4])
        bound = sb("bound", [P, 2])
        top_exp = sb("top_exp", [P, 2])
        half_exp = sb("half_exp", [P, 2], U32)
        sc_exp = sb("sc_exp", [P, 2], U32)
        sc = sb("sc", [P, 2])
        sc2 = sb("sc2", [P, 2])
        epsS = sb("epsS", [P, 2])

        st1a = sb("st1a", [P, TILES, 6])
        mv1a = sb("mv1a", [P, TILES, 2])
        st = sb("st", [P, GT, 6])
        mv = sb("mv", [P, GT, 2])

        def root_work(name):
            return [sb(f"{name}{n}", [P, w])[:, :] for n, w in ((1, TILES), (2, GT))]

        ve, guess, y, yy, rstd = (root_work(n) for n in ("ve", "guess", "y", "yy", "rstd"))
        rstd1, rstd2 = rstd
        nmr1 = sb("nmr1", [P, TILES])
        nmr2 = sb("nmr2", [P, GT])
        xn = sb("xn", [P, GT, D])
        xnT = sb("xnT", [P, GT * P])
        smax = sb("smax", [P, 2, 2])
        nmax = sb("nmax", [P, 2, 2])
        prob = sb("prob", [P, 2, 2, KEYS])
        psum_ = sb("psum_", [P, 2, 2])
        rsum = sb("rsum", [P, 2, 2])
        pT = sb("pT", [P, 2, P])
        xt = sb("xt", [P, GT, D])
        xtT = sb("xtT", [P, GT * P])
        lg = sb("lg", [P, GT, E])
        top = sb("top", [P, TILES, 8])
        topi = sb("topi", [P, GT, 8], U32)
        oh = sb("oh", [P, K, GT, E])
        mask = sb("mask", [P, GT, E], BF16)
        filled = sb("filled", [P, 2, E])
        rank = sb("rank", [P, GT, E])
        pick = sb("pick", [P, K, GT, E])
        posf = sb("posf", [P, K, GT])
        pos = sb("pos", [P, 2, K, GT], U32)
        pay = [sb(f"pay{n}", [P, K, GT, ROW], F16) for n in range(2)]
        gd = sb("gd", [P, TILES])
        ge_ = sb("ge_", [P, TILES])
        gs = sb("gs", [P, TILES])
        gate = sb("gate", [P, K, TILES])

        cnt = sb("cnt", [1, E])
        cnti = sb("cnti", [1, E], I32)
        nti = sb("nti", [1, E], I32)
        ntf = sb("ntf", [1, E])
        ntri = sb("ntri", [1, E, E])
        cum = sb("cum", [1, E])
        full = sb("full", [1, PACKS * PACK, E])
        fulln = sb("fulln", [1, PACKS * PACK, E])
        sx = sb("sx", [1, PACKS * PACK])
        sfirst = sb("sfirst", [1, PACKS * PACK])
        sa = sb("sa", [1, PACKS * PACK])
        sb_ = sb("sb_", [1, PACKS * PACK])
        smin = sb("smin", [1, PACKS * PACK])
        row_tab = sb("row_tab", [1, SLOT_TILES], U32)
        digit = sb("digit", [1, PACKS, PACK])
        packf = sb("packf", [1, PACKS])
        packed = sb("packed", [1, PACKS], U32)
        tail = sb("tail", [1, E], U32)

        NX = 4
        NZ = 3
        xs = [sb(f"xs{n}", [P, ROW], F16) for n in range(NX)]
        xsT = [sb(f"xsT{n}", [P, 2 * P], F16) for n in range(2)]
        r = [cx[:, n * FC:(n + 1) * FC, :].rearrange("p c d -> p (c d)") for n in range(2)]
        rTh = [sb(f"rTh{n}", [P, F], F16) for n in range(2)]
        rTl = [sb(f"rTl{n}", [P, F], F16) for n in range(2)]
        st1 = [sb(f"st1_{n}", [P, 6]) for n in range(4)]
        mv1 = [sb(f"mv1_{n}", [P, 2]) for n in range(4)]
        sd1 = [sb(f"sd1_{n}", [P, 1]) for n in range(4)]
        rs1 = [sb(f"rs1_{n}", [P, 1]) for n in range(4)]
        u, ur = ([cxT[:, n * D:(n + 1) * D] for n in range(at, at + 3)] for at in (0, 3))
        st2 = [sb(f"st2_{n}", [P, 6]) for n in range(4)]
        mv2 = [sb(f"mv2_{n}", [P, 2]) for n in range(4)]
        sd2 = [sb(f"sd2_{n}", [P, 1]) for n in range(4)]
        rs2 = [sb(f"rs2_{n}", [P, 1]) for n in range(4)]
        z0 = [cxT[:, n * D:(n + 1) * D] for n in (6, 7)]
        z1 = [sb(f"z1_{n}", [P, D]) for n in range(2)]
        z = [sb(f"z{n}", [P, D]) for n in range(NZ)]
        ND = 9
        dest = [sb(f"dest{n}", [P, 1], U32) for n in range(ND)]
        def part_c(t, g, n):
            room = n * GT * D
            return t[:, g * room:(g + 1) * room].rearrange("p (k i d) -> p k i d", k=n, i=GT)

        w2_flat = w2f[:, :, :].rearrange("p c d -> p (c d)")
        HG = GROUPS // 2
        ya = [part_c(w1f if g < HG else w2_flat, g % HG, K) for g in range(GROUPS)]
        res = [part_c((w1h if g < HG else w1l)[:, :].bitcast(F32), g % HG, 1)[:, 0, :, :]
               for g in range(GROUPS)]

        def load(name, dst, src, engine="sync"):
            return pr.add(engine, lambda e: e.dma_start(dst, src), signal=signal("ld_" + name), inc=16)

        ev_cx = load("ctx", cx[:, :, :], ctx_in)
        ev_w4 = {}

        def load_w4(q, n, engine):
            ev_w4[n] = load(n, w4[:, q, :], A[f"L0_xattn_{n}"], engine)

        WK, WQ, WV, WO = (w4[:, q, :] for q in range(4))
        load_w4(0, "Wk", "scalar")
        load_w4(1, "Wq", "scalar")
        load_w4(3, "Wo", "sync")
        ev_bq = load("bq", bcol[:, 0:1], A["L0_xattn_bq"].rearrange("(p o) -> p o", o=1))
        ev_x = [load(f"x{g}", x[:, g * GT:(g + 1) * GT, :], x_in[:, g * GT:(g + 1) * GT, :])
                for g in range(GROUPS)]
        H = E // 2
        ev_w1 = [load(f"w1_{h}", w1f[:, h * H * F:(h + 1) * H * F].rearrange("p (e f) -> p e f", e=H),
                      A["L0_ffn_W1"][h * H:(h + 1) * H].rearrange("e d f -> d e f")) for h in range(2)]
        ev_w2 = [load(f"w2_{h}", w2f[:, h * H * FC:(h + 1) * H * FC, :],
                      A["L0_ffn_W2"][h * H:(h + 1) * H].rearrange("e (c p) d -> p (e c) d", p=P))
                 for h in range(2)]

        def flat(name):
            return A[name].rearrange("e f -> (e f)")

        ev_b1 = load("b1", b1c[:, :], flat("L0_ffn_b1").rearrange("(p c) -> p c", p=P))
        ev_gb = [load(n, gb[q * NB:(q + 1) * NB, :], flat("L0_ffn_" + n).rearrange("(c p) -> c p", p=P))
                 for q, n in enumerate(("g1", "be1"))]
        ev_b2 = load("b2", b2row[:, :], flat("L0_ffn_b2").rearrange("(o n) -> o n", o=1))
        ev_g2 = load("g2", g2[:, :], flat("L0_ffn_g2").rearrange("(o n) -> o n", o=1).to_broadcast([P, E * D]))
        ev_be2 = load("be2", be2[:, :], flat("L0_ffn_be2").rearrange("(o n) -> o n", o=1).to_broadcast([P, E * D]))

        s_const = signal("constants")

        def const(issue, after=()):
            return pr.add("gpsimd", issue, after, s_const)

        ev_ones = const(lambda e: e.memset(ones[:, :], 1.0))
        ev_ident = const(lambda e: e.affine_select(out=ident[:, :], in_=ones[:, :], compare_op=ALU.is_equal, fill=0.0,
                                        base=0, pattern=[[-1, P]], channel_multiplier=1), [ev_ones])
        const(lambda e: e.memset(ones16[:, :], 1.0))
        const(lambda e: e.memset(onesb[:, :], 1.0))
        for n in range(2):
            const(lambda e, n=n: e.memset(second[:, n:n + 1], float(n)))
            const(lambda e, n=n: e.affine_select(
                out=pick_row[:, n, :], in_=ones[0:2, :], compare_op=ALU.is_equal, fill=0.0, base=-n,
                pattern=[[0, P]], channel_multiplier=1))
        const(lambda e: e.memset(zero_rows[:, :], 0.0))
        const(lambda e: e.iota(iota_e[:, :, :], [[0, GT], [1, E]], base=0, channel_multiplier=0,
                               allow_small_or_imprecise_dtypes=True))
        const(lambda e: e.iota(trash_row[:, :], [[P, SLOT_TILES]], base=0, channel_multiplier=1,
                               allow_small_or_imprecise_dtypes=True))
        const(lambda e: e.iota(home_row[:, :, :], [[TOKENS, K], [P, TILES]], base=TRASH,
                               channel_multiplier=1))
        const(lambda e: e.iota(slot_no[:, :], [[1, PACKS * PACK]], base=0, channel_multiplier=0,
                               allow_small_or_imprecise_dtypes=True))
        for n in range(2):
            const(lambda e, n=n: e.memset(top_exp[:, n:n + 1], float(BIAS + SC_TOP[n])))
        for k in range(PACK):
            const(lambda e, k=k: e.memset(digit[:, :, k:k + 1], float(F << (BITS * k))))
        for dst in (region0[:, :], filled[:, 0, :]):
            ev_iotas = const(lambda e, dst=dst: e.iota(dst, [[REGION, E]], base=0, channel_multiplier=0,
                                            allow_small_or_imprecise_dtypes=True))
        const(lambda e: e.affine_select(out=ident16[:, :], in_=ones16[:, :], compare_op=ALU.is_equal,
                                        fill=0.0, base=0, pattern=[[-1, P]], channel_multiplier=1), [ev_iotas])
        const(lambda e: e.affine_select(out=below[:, :], in_=onesb[:, :], compare_op=ALU.is_gt, fill=0.0,
                                        base=0, pattern=[[1, P]], channel_multiplier=-1))
        const(lambda e: e.affine_select(out=tri[:, :, :], in_=ones[0:1, 0:E * E].rearrange(
            "p (a b) -> p a b", a=E), compare_op=ALU.is_ge, fill=0.0, base=0, pattern=[[1, E], [-1, E]],
            channel_multiplier=0))
        ev_const = const(lambda e: e.memset(b1t[:, :].bitcast(U32), 0))

        done = {}
        s_pw, s_cw = signal("pe_attn_weights"), signal("copied_attn_weights")

        def pe(issue, after, sig):
            return pr.add("tensor", issue, after, sig)

        def mm(dst, lhsT, rhs, start=True, stop=True):
            return lambda e: e.matmul(dst, lhsT, rhs, start=start, stop=stop)

        def tp(dst, src, idn):
            return lambda e: e.transpose(dst, src, idn)

        def copied(dst, src, after, sig, engine="scalar"):
            issue = (lambda e: e.activation(dst, src, ACT.Copy)) if engine == "scalar" else (
                lambda e: e.tensor_copy(dst, src))
            return pr.add(engine, issue, after, sig)

        b0, b1_ = bank[0:2]
        halves = range(CTX_TILES * P // 512)
        s_ct, s_ctc = signal("pe_ctxT"), signal("copied_ctxT")
        s_kq, s_kqc, s_kbc = signal("pe_keys"), signal("copied_keys"), signal("copied_key_bias")
        s_vo, s_voc = signal("pe_values"), signal("copied_values")
        pr.add("scalar", lambda e: e.activation(kb_col[0:1, :], ones[0:1, 0:1], ACT.Exp), [ev_ones], s_cw)
        load_w4(2, "Wv", "scalar")
        ev_bv = load("bv", bcol[:, 1:2], A["L0_xattn_bv"].rearrange("(p o) -> p o", o=1), "scalar")
        ev_bo = load("bo", borow[:, :], A["L0_xattn_bo"].rearrange("(o n) -> o n", o=1), "scalar")
        ev_wr = load("wr", wr[:, :], A["L0_ffn_Wr"], "scalar")
        ev_br = load("br", brrow[:, :], A["L0_ffn_br"].rearrange("(o n) -> o n", o=1), "scalar")
        def queries_to_keys():
            t = pe(mm(b0[:, D:2 * D], WK, WQ), [ev_w4["Wk"], ev_w4["Wq"]], s_pw)
            yield 0.3
            done["wkq"] = copied(wkq[:, :], b0[:, D:2 * D], [t], s_cw)

        def context(h):
            for c in range(4):
                t = pe(tp(bank[2 + h][:, c * P:(c + 1) * P], cx[:, h * 4 + c, :], ident[:, :]),
                       [ev_cx, ev_ident], s_ct)
            yield 1.0
            done["cxT", h] = copied(cxT[:, h * 512:(h + 1) * 512], bank[2 + h][:, :], [t], s_ctc)

        def out_weights():
            pe(tp(b1_[:, 2 * D:3 * D], WO, ident[:, :]), [ev_w4["Wo"]], s_pw)
            t = pe(mm(b1_[:, 3 * D:3 * D + 1], WK, bcol[:, 0:1]), [ev_bq], s_pw)
            yield 0.7
            copied(woT[:, :], b1_[:, 2 * D:3 * D], [t], s_cw)
            done["woT"] = copied(kb_col[:, :], b1_[:, 3 * D:3 * D + 1], [done["wkq"]], s_cw)

        def keys(h):
            cols_h = slice(h * 512, (h + 1) * 512)
            t = pe(mm(bank[4 + h][:, :], wkq[:, :], cxT[:, cols_h]), [done["cxT", h], done["wkq"]], s_kq)
            yield 1.5
            done["kq"] = copied(kq[:, cols_h], bank[4 + h][:, :], [t], s_kqc)

        def key_bias(h):
            cols_h = slice(h * 512, (h + 1) * 512)
            t = pe(mm(bank[6 + h][0:1, :], kb_col[:, :], cxT[:, cols_h]), [done["cxT", h], done["woT"]], s_kq)
            yield 1.5
            done["kb"] = copied(kb_row[:, cols_h], bank[6 + h][0:1, :], [t], s_kbc)

        def repeat(row, n):
            return row.rearrange("p (a d) -> p a d", a=1).to_broadcast([1, n, row.shape[1]])

        def value_weights():
            pe(mm(b1_[:, 0:D], WV, woT[:, :]), [done["woT"], ev_w4["Wv"]], s_pw)
            pe(mm(b1_[0:1, D:2 * D], bcol[:, 1:2], woT[:, :], stop=False), [ev_bv], s_pw)
            t = pe(mm(b1_[0:1, D:2 * D], ones[0:1, 0:1], borow[:, :], start=False), [ev_bo], s_pw)
            yield 1.2
            copied(wvo[:, :], b1_[:, 0:D], [t], s_cw)
            done["wvo"] = copied(vb_row[:, :], b1_[0:1, D:2 * D], [], s_cw)

        def values(h):
            pe(mm(bank[2 + h][:, :], ones[0:1, :], repeat(vb_row[:, :], 4), stop=False),
               [done["wvo"], done["cxT", h]], s_vo)
            for c in range(4):
                n = h * 4 + c
                t = pe(mm(bank[2 + h][:, c * P:(c + 1) * P], cxT[:, n * P:(n + 1) * P], wvo[:, :],
                          start=False, stop=(c == 3)), [], s_vo)
            yield 2.0
            done["vo"] = copied(vo[:, h * 4:(h + 1) * 4, :],
                                bank[2 + h][:, :].rearrange("p (c d) -> p c d", c=4), [t], s_voc)

        s = {n: signal(n) for n in (
            "stats", "guess", "newton", "nmr", "xn", "pe_xnT", "xnT", "pe_score", "smax", "prob", "rsum",
            "pe_pT", "pT", "pe_attn", "x2", "xt", "pe_xtT", "xtT", "pe_logit", "logit", "top", "pay_hi",
            "pay_lo", "home", "pay_copy", "pe_rank", "rank", "pos", "scatter0", "scatter1")}
        plan = []

        def at(time, step, *args):
            plan.append((time, len(plan), step, args))

        def queue_plan():
            order = dict(key=lambda p: p[:2], reverse=True)
            plan.sort(**order)
            while plan:
                time, n, step, args = plan.pop()
                parts = step(*args) if step is not next else args[0]
                pause = "ended" if parts is None else next(parts, "ended")
                if pause != "ended":
                    plan.append((time + (pause or PACE), n, next, (parts,)))
                    plan.sort(**order)

        def vec(key, issue, after=()):
            return pr.add("vector", issue, after, s[key])

        def act(key, issue, after=()):
            return pr.add("scalar", issue, after, s[key])

        def inverse_root(n, var, after, tiles=slice(0, GT)):
            v, g0, g1_, q = (w[n][:, tiles] for w in (ve, guess, y, yy))
            t = vec("guess", lambda e: e.tensor_scalar(v, var, EPS, None, ALU.add), after)
            yield
            t = vec("guess", lambda e: e.tensor_scalar(g0.bitcast(U32), v.bitcast(U32), 1, None,
                                                       ALU.logical_shift_right), [t])
            yield
            t = vec("guess", lambda e: e.tensor_scalar(g1_.bitcast(U32), g0.bitcast(U32), -1.0,
                                                       float(0x5F3759DF), ALU.mult, ALU.add), [t])
            for k in range(3):
                yield
                dst = rstd[n][:, tiles] if k == 2 else g1_
                t = vec("newton", lambda e: e.tensor_tensor(q, g1_, g1_, ALU.mult), [t])
                yield
                t = vec("newton", lambda e: e.scalar_tensor_tensor(out=g0, in0=q, scalar=-0.5, in1=v,
                                                                   op0=ALU.mult, op1=ALU.mult), [t])
                yield
                t = vec("newton", lambda e, dst=dst: e.scalar_tensor_tensor(
                    out=dst, in0=g0, scalar=1.5, in1=g1_, op0=ALU.add, op1=ALU.mult), [t])
            yield
            return t

        def a_stats1(g):
            for i in range(GT):
                n = g * GT + i
                t = vec("stats", lambda e, n=n: e.bn_stats(st1a[:, n, :], x[:, n, :]), [ev_x[g]])
            yield
            for i in range(GT):
                n = g * GT + i
                t2 = vec("stats", lambda e, n=n: e.bn_aggr(mv1a[:, n, :], st1a[:, n, :]), [t])
            done["stats1", g] = t2

        def a_rstd1(first, end):
            tiles = slice(first * GT, end * GT)
            t = yield from inverse_root(0, mv1a[:, tiles, 1], [done["stats1", g] for g in range(first, end)], tiles)
            t = vec("nmr", lambda e: e.scalar_tensor_tensor(
                out=nmr1[:, tiles], in0=mv1a[:, tiles, 0], scalar=-1.0, in1=rstd1[:, tiles], op0=ALU.mult,
                op1=ALU.mult), [t])
            for g in range(first, end):
                done["nmr1", g] = t

        def a_xn(g):
            for i in range(GT):
                n = g * GT + i
                done["xn", g] = act("xn", lambda e, i=i, n=n: e.activation(
                    xn[:, i, :], x[:, n, :], ACT.Identity, bias=nmr1[:, n:n + 1], scale=rstd1[:, n:n + 1]),
                    [done["nmr1", g], done.get(("pe_xnT", g - 1))])

        def a_xnT(g):
            for i in range(GT):
                t = pe(tp(bank[0][:, i * P:(i + 1) * P], xn[:, i, :], ident[:, :]),
                       [done["xn", g], done.get(("xnT", g - 1))], s["pe_xnT"])
            done["pe_xnT", g] = t

        def a_xnT_copy(g):
            done["xnT", g] = act("xnT", lambda e: e.activation(xnT[:, :], bank[0][:, :], ACT.Copy),
                                 [done["pe_xnT", g], done.get(("pe_score", g - 1))])

        scores = bank[1][:, 0:4 * KEYS].rearrange("p (q b k) -> p q b k", q=2, b=2)

        def a_score(g):
            pair = slice(2 * g * KEYS, (2 * g + 2) * KEYS)
            pe(mm(bank[1][:, 0:4 * KEYS], ones[0:1, :], repeat(kb_row[:, pair], 2), stop=False),
               [done["xnT", g], done["kq"], done["kb"], done["wvo"], done.get(("prob", g - 1))], s["pe_score"])
            for i in range(GT):
                b, q = i // 2, i % 2
                keys = slice((2 * g + b) * KEYS, (2 * g + b + 1) * KEYS)
                dst = bank[1][:, (2 * q + b) * KEYS:(2 * q + b + 1) * KEYS]
                t = pe(mm(dst, xnT[:, i * P:(i + 1) * P], kq[:, keys], start=False, stop=(i == GT - 1)), [],
                       s["pe_score"])
            done["pe_score", g] = t

        def a_max(g):
            t = vec("smax", lambda e: e.tensor_reduce(smax[:, :, :], scores, AX.X, ALU.max),
                    [done["pe_score", g]])
            yield
            done["smax", g] = vec("smax", lambda e: e.tensor_scalar(
                nmax[:, :, :], smax[:, :, :], -SCALE, None, ALU.mult), [t, done.get(("prob", g - 1))])

        def a_prob(g):
            for q in range(2):
                for b in range(2):
                    t = act("prob", lambda e, q=q, b=b: e.activation(
                        prob[:, q, b, :], scores[:, q, b, :], ACT.Exp, bias=nmax[:, q, b:b + 1], scale=SCALE,
                        accum_out=psum_[:, q, b:b + 1]),
                        [done["smax", g], done.get(("pe_pT", g - 1)), done.get(("rsum", g - 1))])
            done["prob", g] = t

        def a_rsum(g):
            done["rsum", g] = vec("rsum", lambda e: e.reciprocal(rsum[:, :, :], psum_[:, :, :]),
                                  [done["prob", g], done.get(("x2", g - 1))])

        def a_pT(g):
            for q in range(2):
                t = pe(tp(bank[2][:, q * P:(q + 1) * P],
                          prob[:, q, :, :].rearrange("p b k -> p (b k)"), ident[:, :]),
                       [done["prob", g], done["vo"], done.get(("pT", g - 1))], s["pe_pT"])
            done["pe_pT", g] = t

        def a_pT_copy(g):
            done["pT", g] = act("pT", lambda e: e.activation(
                pT[:, :, :], bank[2][:, 0:2 * P].rearrange("p (q k) -> p q k", q=2), ACT.Copy),
                [done["pe_pT", g], done.get(("pe_attn", g - 1))])

        def attn(b, q):
            return bank[3 + 4 * b][:, q * D:(q + 1) * D]

        def a_attend(g):
            for i in range(GT):
                b, q = i // 2, i % 2
                rows = slice(b * KEYS, (b + 1) * KEYS)
                t = pe(mm(attn(b, q), pT[rows, q, :], vo[rows, g, :]),
                       [done["pT", g], done["kq"], done.get(("x2", g - 1))], s["pe_attn"])
            done["pe_attn", g] = t

        def a_x2(g):
            for i in range(GT):
                b, q = i // 2, i % 2
                t = vec("x2", lambda e, i=i, b=b, q=q: e.scalar_tensor_tensor(
                    out=x2[:, g * GT + i, :], in0=attn(b, q), scalar=rsum[:, q, b:b + 1],
                    in1=x[:, g * GT + i, :], op0=ALU.mult, op1=ALU.add), [done["pe_attn", g], done["rsum", g]])
                if i < GT - 1:
                    yield
            done["x2", g] = t

        def a_stats2(g):
            for i in range(GT):
                t = vec("stats", lambda e, i=i: e.bn_stats(st[:, i, :], x2[:, g * GT + i, :]), [done["x2", g]])
            yield
            for i in range(GT):
                t2 = vec("stats", lambda e, i=i: e.bn_aggr(mv[:, i, :], st[:, i, :]), [t])
            done["stats2", g] = t2

        def a_rstd2(g):
            t = yield from inverse_root(1, mv[:, :, 1], [done["stats2", g], done.get(("xt", g - 1))])
            done["nmr2", g] = vec("nmr", lambda e: e.scalar_tensor_tensor(
                out=nmr2[:, :], in0=mv[:, :, 0], scalar=-1.0, in1=rstd2, op0=ALU.mult, op1=ALU.mult),
                [t])

        def a_xt(g):
            for i in range(GT):
                done["xt", g] = act("xt", lambda e, i=i: e.activation(
                    xt[:, i, :], x2[:, g * GT + i, :], ACT.Identity, bias=nmr2[:, i:i + 1],
                    scale=rstd2[:, i:i + 1]),
                    [done["nmr2", g], done.get(("pe_xtT", g - 1)), done.get(("pay_lo", g - 1))])

        def a_xtT(g):
            for i in range(GT):
                t = pe(tp(bank[4][:, i * P:(i + 1) * P], xt[:, i, :], ident[:, :]),
                       [done["xt", g], done.get(("xtT", g - 1))], s["pe_xtT"])
            done["pe_xtT", g] = t

        def a_xtT_copy(g):
            done["xtT", g] = act("xtT", lambda e: e.activation(xtT[:, :], bank[4][:, :], ACT.Copy),
                                 [done["pe_xtT", g], done.get(("pe_logit", g - 1))])

        def a_logit(g):
            pe(mm(bank[5][:, 0:GT * E], ones[0:1, :], repeat(brrow[:, :], GT), stop=False),
               [done["xtT", g], ev_wr, ev_br, done.get(("rank", g - 1))], s["pe_logit"])
            for i in range(GT):
                t = pe(mm(bank[5][:, i * E:(i + 1) * E], xtT[:, i * P:(i + 1) * P], wr[:, :], start=False,
                          stop=(i == GT - 1)), [], s["pe_logit"])
            done["pe_logit", g] = t

        def a_logit_copy(g):
            done["logit", g] = vec("logit", lambda e: e.tensor_copy(
                lg[:, :, :], bank[5][:, 0:GT * E].rearrange("p (i e) -> p i e", i=GT)), [done["pe_logit", g]])

        def a_pay_hi(g):
            done["pay_hi", g] = act("pay_hi", lambda e: e.activation(
                pay[g % 2][:, 0, :, 0:D], xt[:, :, :], ACT.Copy), [done["xt", g], done.get(("scatter", g - 2))])

        def a_pay_lo(g):
            p = pay[g % 2]
            done["pay_lo", g] = t = vec("pay_lo", lambda e: e.tensor_tensor(
                p[:, 0, :, D:2 * D], xt[:, :, :], p[:, 0, :, 0:D], ALU.subtract), [done["pay_hi", g]])
            done["home", g] = vec("home", lambda e: e.tensor_copy(
                p[:, :, :, 2 * D:2 * D + 2].bitcast(U32)[:, :, :, 0], home_row[:, :, g * GT:(g + 1) * GT]),
                [ev_const])

        def a_pay_copy(g):
            p = pay[g % 2]
            done["pay", g] = act("pay_copy", lambda e: e.activation(
                p[:, 1, :, 0:2 * D], p[:, 0, :, 0:2 * D], ACT.Copy), [done["pay_lo", g]])

        def a_top(g):
            for i in range(GT):
                t = vec("top", lambda e, i=i: e.max(top[:, g * GT + i, :], lg[:, i, :]), [done["logit", g]])
            yield
            for i in range(GT):
                t2 = vec("top", lambda e, i=i: e.max_index(topi[:, i, :], top[:, g * GT + i, :], lg[:, i, :]),
                         [t])
            yield
            for k in range(K):
                t = vec("top", lambda e, k=k: e.tensor_tensor(
                    oh[:, k, :, :], iota_e[:, :, :], topi[:, :, k:k + 1].to_broadcast([P, GT, E]),
                    ALU.is_equal), [t2, ev_const])
            yield
            done["mask", g] = vec("top", lambda e: e.tensor_tensor(
                mask[:, :, :], oh[:, 0, :, :], oh[:, 1, :, :], ALU.add), [t])

        def a_rank(g):
            m = mask[:, :, :].rearrange("p i e -> p (i e)")
            pe(mm(bank[5][:, 64:64 + GT * E], below[:, :], m, stop=False), [done["mask", g]], s["pe_rank"])
            for d in range(1, GT):
                pe(mm(bank[5][:, 64 + d * E:64 + GT * E], onesb[:, :], m[:, 0:(GT - d) * E], start=False,
                      stop=(d == GT - 1)), [], s["pe_rank"])
            for i in range(GT):
                t = pe(mm(bank[5][:, 128:128 + E], onesb[:, :], m[:, i * E:(i + 1) * E], start=(i == 0),
                          stop=(i == GT - 1)), [], s["pe_rank"])
            done["pe_rank", g] = t

        def a_pos(g):
            c, nx = g % 2, (g + 1) % 2
            vec("rank", lambda e: e.tensor_tensor(
                rank[:, :, :], bank[5][:, 64:64 + GT * E].rearrange("p (i e) -> p i e", i=GT),
                filled[:, c:c + 1, :].to_broadcast([P, GT, E]), ALU.add),
                [done["pe_rank", g], done.get(("rank", g - 1))])
            done["rank", g] = t = vec("rank", lambda e: e.tensor_tensor(
                filled[:, nx, :], bank[5][:, 128:128 + E], filled[:, c, :], ALU.add))
            yield
            for k in range(K):
                t2 = vec("pos", lambda e, k=k: e.tensor_tensor(pick[:, k, :, :], oh[:, k, :, :],
                                                               rank[:, :, :], ALU.mult), [t])
            yield
            t = vec("pos", lambda e: e.tensor_reduce(posf[:, :, :], pick[:, :, :, :], AX.X, ALU.add), [t2])
            yield
            done["pos", g] = vec("pos", lambda e: e.tensor_copy(pos[:, g % 2, :, :], posf[:, :, :]),
                                 [t, done.get(("scatter", g - 2))])

        def a_scatter(g, k, i):
            done["scatter", g] = pr.add("gpsimd", lambda e: e.indirect_dma_start(
                slots, bass.IndirectOffsetOnAxis(ap=pos[:, g % 2, k, i:i + 1], axis=0),
                pay[g % 2][:, k, i, :], None), [done["pos", g], done["pay" if k else "pay_lo", g],
                                                          done["home", g]], s[f"scatter{g % 2}"], 16)

        s_scale, s_sp, s_squares = signal("scale"), signal("pe_scale"), signal("squares")

        def square_sum(col, src, room, after):
            done["ss", col] = pr.add("scalar", lambda e: e.activation(
                room, src, ACT.Square, accum_out=ss[:, col:col + 1]), after, s_squares)

        w2_all = w2f[:, :, :].rearrange("p c d -> p (c d)")

        def gains():
            t = pe(tp(bank[6][:, 0:2 * NB], gb[:, :], ident[0:2 * NB, 0:2 * NB]), [*ev_gb, done["kb"]], s_sp)
            yield 0.3
            ev_g1 = copied(gbT[:, :], bank[6][:, 0:2 * NB], [t], s_scale, "vector")
            pr.add("vector", lambda e: e.tensor_scalar(gm[:, :, 0], bank[6][:, 0:NB], 1.0 / F, None, ALU.mult),
                   [], s_scale)
            done["gm"] = done["bank6"] = copied(gm[:, :, 1], bank[6][:, NB:2 * NB], [], s_scale, "vector")
            t = pr.add("vector", lambda e: e.tensor_reduce(gmax[:, :], g1c[:, :], AX.X, ALU.max,
                                                           apply_absolute_value=True), [ev_g1], s_scale)
            yield
            done["ss", 3] = pr.add("vector", lambda e: e.tensor_tensor(ss[:, 3:4], gmax[:, :], gmax[:, :],
                                                                       ALU.mult), [t], s_scale)

        def weight_scale():
            def dv(issue, after):
                return pr.add("vector", issue, after, s_scale)
            t = pe(mm(bank[6][:, 0:4], ones[:, :], ss[:, :]),
                   [*(done["ss", n] for n in range(4)), done["bank6"]], s_sp)
            t = done["bank6"] = dv(lambda e: e.tensor_copy(total[:, :], bank[6][:, 0:4]), [t])
            yield
            dv(lambda e: e.tensor_tensor(bound[:, 0:1], total[:, 0:1], total[:, 1:2], ALU.add), [t])
            t = dv(lambda e: e.tensor_tensor(bound[:, 1:2], total[:, 2:3], total[:, 3:4], ALU.mult), [])
            yield
            t = dv(lambda e: e.tensor_scalar(bound[:, :], bound[:, :], 1e-24, 1e36, ALU.max, ALU.min), [t])
            yield
            t = dv(lambda e: e.tensor_scalar(half_exp[:, :], bound[:, :].bitcast(U32), MANTISSA + 1, None,
                                             ALU.logical_shift_right), [t])
            yield
            t = dv(lambda e: e.tensor_tensor(sc_exp[:, :], top_exp[:, :], half_exp[:, :], ALU.subtract),
                   [t, ev_const])
            yield
            t = dv(lambda e: e.tensor_scalar(sc[:, :].bitcast(U32), sc_exp[:, :], MANTISSA, None,
                                             ALU.logical_shift_left), [t])
            yield
            t = dv(lambda e: e.tensor_tensor(sc2[:, :], sc[:, :], sc[:, :], ALU.mult), [t])
            yield
            done["scale"] = dv(lambda e: e.tensor_scalar(epsS[:, :], sc2[:, :], EPS, None, ALU.mult), [t])
            yield
            t = dv(lambda e: e.tensor_scalar(b1h[:, :], b1c[:, :], sc[:, 0:1], None, ALU.mult),
                   [done["scale"]])
            yield
            t = dv(lambda e: e.scalar_tensor_tensor(out=b1l[:, :], in0=b1c[:, :], scalar=sc[:, 0:1],
                                                    in1=b1h[:, :], op0=ALU.mult, op1=ALU.subtract), [t])
            s_b1 = signal("b1_rows")
            for n, src in enumerate((b1h, b1l)):
                done["b1t"] = pr.add("sync", lambda e, n=n, src=src: e.dma_start(
                    b1t[n:n + 1, :].rearrange("o (p c) -> o p c", p=P), src[:, :]), [t, ev_const], s_b1, 16)

        s_w = {n: signal(n) for n in ("w_hi", "w_lo", "w2g", "w2c", "pe_rows", "rows", "pe_mean", "mean", "pe_c2", "c2")}

        def cols(t, e_):
            return t[:, e_ * F:(e_ + 1) * F]

        def chunks(t, e_):
            return cols(t, e_).rearrange("p (c d) -> p c d", c=FC)

        def w_up(e_):
            t = pr.add("scalar", lambda e: e.activation(cols(w1h, e_), cols(w1f, e_), ACT.Copy,
                                                        scale=sc[:, 0:1]), [done["scale"]], s_w["w_hi"])
            done["w1h", e_] = t

        def w_up_lo(e_):
            pr.add("vector", lambda e: e.scalar_tensor_tensor(
                out=cols(w1l, e_), in0=cols(w1f, e_), scalar=sc[:, 0:1], in1=cols(w1h, e_), op0=ALU.mult,
                op1=ALU.subtract), [done["w1h", e_]], s_w["w_lo"])

        def half(t, h):
            return t[:, h * H * D:(h + 1) * H * D]

        def w_rows(h):
            t = pe(mm(bank[6][0:2, :], second[:, :], half(b2row, h), stop=False),
                   [ev_b2, ev_w2[h], done["gm"], done.get("bank6"), ev_const], s_w["pe_rows"])
            for n in range(h * H * FC, (h + 1) * H * FC):
                at_d = (n // FC) % H * D
                t = pe(mm(bank[6][0:2, at_d:at_d + D], gm[:, n, :], w2f[:, n, :], start=False,
                          stop=(n % (H * FC) == H * FC - 1)), [], s_w["pe_rows"])
                if n % FC == FC - 1:
                    yield 1.7
            done["rows", h] = done["bank6"] = copied(half(w2_rows, h), bank[6][0:2, :], [t], s_w["rows"])

        def w_mean(h):
            t = pe(mm(bank[6][:, :], pick_row[:, 0, :], half(w2_rows, h)), [done["bank6"]], s_w["pe_mean"])
            yield 1.5
            done["mean", h] = done["bank6"] = copied(half(w2_mean, h), bank[6][:, :], [t], s_w["mean"])

        def w_offset(h):
            t = pe(mm(bank[6][:, :], pick_row[:, 1, :], half(w2_rows, h)), [done["bank6"], done["scale"]],
                   s_w["pe_c2"])
            yield 1.5
            done["c2"] = done["bank6"] = pr.add("scalar", lambda e: e.activation(
                half(c2, h), bank[6][:, :], ACT.Copy, scale=sc[:, 1:2]), [t], s_w["c2"])

        def w_gained(e_):
            for c in range(FC):
                n = e_ * FC + c
                done["w2g", e_] = pr.add("scalar", lambda e, n=n, c=c: e.activation(
                    w2g[:, c, :], w2f[:, n, :], ACT.Copy, scale=g1c[:, n:n + 1]),
                    [done["gm"], done.get(("w2c", e_ - 1))], s_w["w2g"])

        def w_centred(e_):
            done["w2c", e_] = pr.add("vector", lambda e: e.tensor_tensor(
                w2c[:, :, :], w2g[:, :, :], w2_mean[:, e_ * D:(e_ + 1) * D].rearrange(
                    "p (c d) -> p c d", c=1).to_broadcast([P, FC, D]), ALU.subtract),
                [done["w2g", e_], done["mean", e_ // H], done.get(("w_lo2", e_ - 1))], s_w["w2c"])

        def w_down(e_):
            done["w2h", e_] = pr.add("scalar", lambda e: e.activation(
                chunks(w2h, e_), w2c[:, :, :], ACT.Copy, scale=sc[:, 1:2]),
                [done["w2c", e_], done["scale"]], s_w["w_hi"])

        def w_down_lo(e_):
            done["w_lo2", e_] = pr.add("vector", lambda e: e.scalar_tensor_tensor(
                out=chunks(w2l, e_), in0=w2c[:, :, :], scalar=sc[:, 1:2], in1=chunks(w2h, e_),
                op0=ALU.mult, op1=ALU.subtract), [done["w2h", e_]],
                s_w["w_lo"])

        s_tab, s_zero = signal("tables"), signal("zeroed")
        s_g, s_ge = signal("gates"), signal("gate_exp")

        def zero_tail(e_):
            def issue(eng):
                row = eng.value_load(tail[0:1, e_:e_ + 1], min_val=e_ * REGION, max_val=e_ * REGION + TOKENS)
                return eng.dma_start(slots[bass.ds(row, P), :], zero_rows[:, :])
            return issue

        def zero_tails():
            pr.add("sync", lambda e: e.dma_start(slots[E * REGION:, :], zero_rows[:, :]), [ev_const], s_zero, 16)
            for e_ in range(E):
                done["zeroed"] = pr.add("sync", zero_tail(e_), [done["tail"]], s_zero, 16)

        def tables():
            def tab(issue, after=()):
                return pr.add("vector", issue, after, s_tab)

            def as_row(ap, n):
                return ap.rearrange("p (a e) -> p a e", a=1).to_broadcast([1, n, E])

            n_tab, end = PACKS * PACK, filled[0:1, GROUPS % 2, :]
            done["tail"] = tab(lambda e: e.tensor_copy(tail[:, :], end), [done["rank", GROUPS - 1]])
            t = tab(lambda e: e.tensor_tensor(cnt[:, :], end, region0[0:1, :], ALU.subtract))
            yield
            t = tab(lambda e: e.tensor_scalar(cnti[:, :], cnt[:, :], float(P - 1), None, ALU.add), [t])
            yield
            t = tab(lambda e: e.tensor_scalar(nti[:, :], cnti[:, :], P.bit_length() - 1, None,
                                              ALU.arith_shift_right), [t])
            yield
            t = tab(lambda e: e.tensor_copy(ntf[:, :], nti[:, :]), [t])
            yield
            t = tab(lambda e: e.tensor_tensor(ntri[:, :, :], tri[:, :, :], as_row(ntf[:, :], E), ALU.mult), [t])
            yield
            t = tab(lambda e: e.tensor_reduce(cum[:, :], ntri[:, :, :], AX.X, ALU.add), [t])
            yield
            t = tab(lambda e: e.tensor_tensor(
                full[:, :, :], as_row(cum[:, :], n_tab),
                slot_no[:, :].rearrange("p (j a) -> p j a", a=1).to_broadcast([1, n_tab, E]), ALU.is_le), [t])
            yield
            t = tab(lambda e: e.tensor_reduce(sx[:, :], full[:, :, :], AX.X, ALU.add), [t])
            tab(lambda e: e.tensor_tensor(fulln[:, :, :], full[:, :, :], as_row(ntf[:, :], n_tab), ALU.mult))
            yield
            t = tab(lambda e: e.scalar_tensor_tensor(
                out=smin[:, :], in0=sx[:, :], scalar=float(E - 1),
                in1=digit[:, :, :].rearrange("p a k -> p (a k)"), op0=ALU.min, op1=ALU.mult), [t])
            yield
            t = tab(lambda e: e.tensor_reduce(sfirst[:, :], fulln[:, :, :], AX.X, ALU.add), [t])
            tab(lambda e: e.tensor_reduce(packf[:, :], smin[:, :].rearrange("p (a k) -> p a k", k=PACK), AX.X,
                                          ALU.add))
            yield
            t = tab(lambda e: e.tensor_tensor(sa[:, :], slot_no[:, :], sfirst[:, :], ALU.subtract), [t])
            t = tab(lambda e: e.tensor_scalar(sb_[:, :], sx[:, :], float(REGION), None, ALU.mult))
            yield
            t = tab(lambda e: e.scalar_tensor_tensor(out=sa[:, :], in0=sa[:, :], scalar=float(P), in1=sb_[:, :],
                                                     op0=ALU.mult, op1=ALU.add), [t])
            tab(lambda e: e.tensor_copy(packed[:, :], packf[:, :]))
            yield
            done["tables"] = tab(lambda e: e.tensor_scalar(row_tab[:, :], sa[:, 0:SLOT_TILES],
                                                           float(E * REGION), None, ALU.min), [t])

        def gates():
            t = pr.add("vector", lambda e: e.tensor_tensor(gd[:, :], top[:, :, 1], top[:, :, 0],
                                                           ALU.subtract), [done["mask", GROUPS - 1]], s_g)
            yield
            t = pr.add("scalar", lambda e: e.activation(ge_[:, :], gd[:, :], ACT.Exp), [t], s_ge)
            pr.add("scalar", lambda e: e.activation(gs[:, 0:1], ones[:, 0:1], ACT.Sqrt), [], s_ge)
            yield 1.5
            t = pr.add("vector", lambda e: e.tensor_scalar(gs[:, :], ge_[:, :], 1.0, None, ALU.add),
                       [(s_ge, s_ge.count)], s_g)
            yield
            t = pr.add("vector", lambda e: e.reciprocal(gate[:, 0, :], gs[:, :]), [t], s_g)
            yield
            done["gate"] = pr.add("vector", lambda e: e.tensor_tensor(gate[:, 1, :], ge_[:, :], gate[:, 0, :],
                                                                      ALU.mult), [t], s_g)

        for time, step, *args in ((-105.2, a_stats1, 0), (-99.6, a_stats1, 1), (-97.6, queries_to_keys),
                                  (-86.6, context, 0), (-79.5, a_rstd1, 0, 2), (-68.6, a_stats1, 3),
                                  (-64.3, context, 1), (-61.0, keys, 0), (-59.2, a_stats1, 6),
                                  (-58.3, out_weights), (-45.8, keys, 1), (-45.4, a_stats1, 2),
                                  (-44.0, a_stats1, 5), (-29.7, value_weights), (-14.3, a_stats1, 7),
                                  (-13.0, key_bias, 0), (-10.2, key_bias, 1), (-8.9, a_stats1, 4),
                                  (-5.2, values, 1), (1.1, values, 0), (1.5, a_rstd1, 2, GROUPS),
                                  (5.2, gains), (9.1, square_sum, 0, w1f[:, :], w1h[:, :], ev_w1),
                                  (22.1, square_sum, 1, b1c[:, :], b1h[:, :], [ev_b1]), (24.3, w_rows, 0),
                                  (27.3, square_sum, 2, w2_all, w2h[:, :], ev_w2), (33.1, w_mean, 0),
                                  (36.3, weight_scale), (79.8, w_rows, 1), (86.9, w_mean, 1),
                                  (93.6, w_offset, 0), (174.7, w_offset, 1)):
            at(time, step, *args)
        starts = (-13.0, -3.1, 6.8, 16.7, 26.5, 36.4, 46.3, 56.2)
        for g, start in enumerate(starts):
            for time, step in ((0.0, a_xn), (4.8, a_xnT), (7.64, a_xnT_copy), (11.9, a_score),
                               (14.88, a_max), (15.9, a_prob), (17.15, a_pT), (18.97, a_pT_copy),
                               (20.38, a_attend), (20.97, a_rsum), (21.04, a_x2), (23.54, a_stats2),
                               (24.62, a_rstd2), (28.88, a_xt), (30.5, a_xtT), (30.72, a_xtT_copy),
                               (31.54, a_pay_hi), (33.96, a_logit), (35.05, a_pay_lo),
                               (35.34, a_logit_copy), (35.55, a_top), (38.16, a_rank), (39.74, a_pos),
                               (44.23, a_pay_copy)):
                at(start + time, step, g)
            for n in range(K * GT):
                at(start + 42.58 + 1.04 * n, a_scatter, g, n // GT, n % GT)
        starts = (69.0, 79.8, 90.6, 101.4, 112.2, 123.0, 133.8, 147.5)
        for e_, start in enumerate(starts):
            for time, step in ((-27.37, w_gained), (-20.86, w_centred), (-17.67, w_down),
                               (-13.4, w_down_lo), (0.0, w_up), (4.39, w_up_lo)):
                at(start + time, step, e_)
        at(96.8, tables)
        at(96.9, zero_tails)
        at(92.7, gates)
        queue_plan()

        s.update({n: signal(n) for n in (
            "pe_xsT", "xsT", "pe_h", "relu1", "bstats1", "std1", "rstd1", "pe_rT", "rT_hi", "rT_lo", "pe_y",
            "affine", "relu2", "bstats2", "std2", "rstd2", "z0", "z", "dest")})
        s_rows = [signal(f"rows{n}") for n in range(NX)]
        s_ans = [signal(f"answer{n}") for n in range(NZ)]
        scattered = [done["scatter", GROUPS - 1], done["scatter", GROUPS - 2]]
        psX, psH, psT, psY = bank[0:2], bank[2:4], bank[4:6], bank[6:8]
        regs = {}

        def b_pack(q, name):
            def issue(eng):
                regs[name, q] = eng.value_load(packed[0:1, q:q + 1], min_val=0,
                                                       max_val=F * ((1 << (BITS * PACK)) - 1))
            pr.add(name, issue, [done["tables"]])

        def column(eng, name, j, width):
            drop = BITS * (j % PACK) + (F // width).bit_length() - 1
            return eng.snap((regs[name, j // PACK] >> drop) & ((E - 1) * width), min_val=0,
                            max_val=(E - 1) * width)

        def b_load(j):
            def issue(eng):
                row = eng.value_load(row_tab[0:1, j:j + 1], min_val=0, max_val=E * REGION)
                return eng.dma_start(xs[j % NX][:, :], slots[bass.ds(row, P), :])
            done["rows", j] = pr.add("sync", issue, [done["tables"], done["zeroed"], *scattered,
                                                     done.get(("pe_xsT", j - NX)), done.get(("dest", j - NX))],
                                     s_rows[j % NX], 16)

        def turned(j):
            return psX[j % 2][:, 0:P].bitcast(F16)

        def b_turn(j):
            for n in range(2):
                t = pe(tp(turned(j)[:, n * P:(n + 1) * P], xs[j % NX][:, n * D:(n + 1) * D], ident16[:, :]),
                       [done["rows", j], done.get(("xsT", j - 2)), done.get("phase")], s["pe_xsT"])
            done["pe_xsT", j] = t

        def b_turn_copy(j):
            done["xsT", j] = act("xsT", lambda e: e.activation(xsT[j % 2][:, :], turned(j), ACT.Copy),
                                 [done["pe_xsT", j], done.get(("pe_h", j - 2))])

        def b_dest(j):
            done["dest", j] = vec("dest", lambda e: e.tensor_tensor(
                dest[j % ND][:, :], xs[j % NX][:, 2 * D:2 * D + 2].bitcast(U32), trash_row[:, j:j + 1],
                ALU.max), [done["rows", j], done.get(("answer", j - ND))])

        def b_up(j):
            hi, lo = xsT[j % 2][:, 0:P], xsT[j % 2][:, P:2 * P]
            dst = psH[j % 2][:, :]

            def issue(eng):
                off = regs["column", j] = column(eng, "tensor", j, F)
                w = lambda t: t[:, bass.ds(off, F)]
                eng.matmul(dst, ones16[:, :], w(b1t), start=True, stop=False)
                eng.matmul(dst, hi, w(w1h), start=False, stop=False)
                eng.matmul(dst, hi, w(w1l), start=False, stop=False)
                return eng.matmul(dst, lo, w(w1h), start=False, stop=True)
            done["pe_h", j] = pe(issue, [done["xsT", j], done.get(("relu1", j - 2)), done["b1t"],
                                         done["w_lo2", E - 1], done["tables"]], s["pe_h"])

        def b_relu(j):
            done["relu1", j] = act("relu1", lambda e: e.activation(r[j % 2][:, :], psH[j % 2][:, :], ACT.Relu),
                                   [done["pe_h", j], done.get(("pe_rT", j - 2)), done.get(("bstats1", j - 2))])

        def b_stats(j):
            done["bstats1", j] = vec("bstats1", lambda e: e.bn_stats(st1[j % 4][:, :], r[j % 2][:, :]),
                                     [done["relu1", j]])

        def b_aggr(j):
            done["aggr1", j] = vec("bstats1", lambda e: e.bn_aggr(mv1[j % 4][:, :], st1[j % 4][:, :]),
                                   [done["bstats1", j]])

        def b_std(j):
            done["std1", j] = act("std1", lambda e: e.activation(
                sd1[j % 4][:, :], mv1[j % 4][:, 1:2], ACT.Sqrt, bias=epsS[:, 0:1]), [done["aggr1", j]])

        def b_rstd(j):
            done["rstd1", j] = vec("rstd1", lambda e: e.reciprocal(rs1[j % 4][:, :], sd1[j % 4][:, :]),
                                   [done["std1", j]])

        def b_turn_r(j):
            for c in range(FC):
                t = pe(tp(psT[j % 2][:, c * P:(c + 1) * P], r[j % 2][:, c * P:(c + 1) * P], ident[:, :]),
                       [done["relu1", j], done.get(("rT_lo", j - 2))], s["pe_rT"])
            done["pe_rT", j] = t

        def b_rT_hi(j):
            done["rT_hi", j] = act("rT_hi", lambda e: e.activation(rTh[j % 2][:, :], psT[j % 2][:, :], ACT.Copy),
                                   [done["pe_rT", j], done.get(("pe_y", j - 2))])

        def b_rT_lo(j):
            done["rT_lo", j] = vec("rT_lo", lambda e: e.tensor_tensor(
                rTl[j % 2][:, :], psT[j % 2][:, :], rTh[j % 2][:, :], ALU.subtract), [done["rT_hi", j]])

        def b_down(j):
            dst = psY[j % 2][:, 0:D]

            def issue(eng):
                off = regs["column", j]
                for c in range(FC):
                    hi, lo = (t[j % 2][:, c * P:(c + 1) * P] for t in (rTh, rTl))
                    wh, wl = (t[:, bass.ds(off + c * D, D)] for t in (w2h, w2l))
                    eng.matmul(dst, hi, wh, start=(c == 0), stop=False)
                    eng.matmul(dst, hi, wl, start=False, stop=False)
                    ins = eng.matmul(dst, lo, wh, start=False, stop=(c == FC - 1))
                return ins
            done["pe_y", j] = pe(issue, [done["rT_lo", j], done.get(("affine", j - 2))], s["pe_y"])

        def b_affine(j):
            def issue(eng):
                off = column(eng, "vector", j, D)
                return eng.scalar_tensor_tensor(out=u[j % 3][:, :], in0=psY[j % 2][:, 0:D],
                                                scalar=rs1[j % 4][:, 0:1], in1=c2[:, bass.ds(off, D)],
                                                op0=ALU.mult, op1=ALU.add)
            done["affine", j] = vec("affine", issue, [done["pe_y", j], done["rstd1", j], done["c2"],
                                                      done.get(("relu2", j - 3))])

        def b_relu2(j):
            done["relu2", j] = act("relu2", lambda e: e.activation(ur[j % 3][:, :], u[j % 3][:, :], ACT.Relu),
                                   [done["affine", j], done.get(("z0", j - 3))])

        def b_stats2(j):
            done["bstats2", j] = vec("bstats2", lambda e: e.bn_stats(st2[j % 4][:, :], ur[j % 3][:, :]),
                                     [done["relu2", j]])

        def b_aggr2(j):
            done["aggr2", j] = vec("bstats2", lambda e: e.bn_aggr(mv2[j % 4][:, :], st2[j % 4][:, :]),
                                   [done["bstats2", j]])

        def b_std2(j):
            done["std2", j] = act("std2", lambda e: e.activation(
                sd2[j % 4][:, :], mv2[j % 4][:, 1:2], ACT.Sqrt, bias=epsS[:, 1:2]), [done["aggr2", j]])

        def b_rstd2(j):
            done["rstd2", j] = vec("rstd2", lambda e: e.reciprocal(rs2[j % 4][:, :], sd2[j % 4][:, :]),
                                   [done["std2", j]])

        def b_norm(j):
            done["z0", j] = vec("z0", lambda e: e.tensor_scalar(
                z0[j % 2][:, :], ur[j % 3][:, :], mv2[j % 4][:, 0:1], rs2[j % 4][:, 0:1], ALU.subtract,
                ALU.mult), [done["rstd2", j], done.get(("z1", j - 2))])

        def b_out(j):
            pool = lambda issue, after=(): pr.add("gpsimd", issue, after, s["z"])

            def scaled(eng):
                off = regs["row", j] = column(eng, "gpsimd", j, D)
                return eng.tensor_tensor(z1[j % 2][:, :], z0[j % 2][:, :], g2[:, bass.ds(off, D)], ALU.mult)
            t = done["z1", j] = pool(scaled, [done["z0", j], ev_g2, ev_be2, done["tables"]])
            done["z", j] = pool(lambda e: e.tensor_tensor(
                z[j % NZ][:, :], z1[j % 2][:, :], be2[:, bass.ds(regs["row", j], D)], ALU.add),
                [t, done.get(("answer", j - NZ))])

        def b_answer(j):
            done["answer", j] = pr.add("gpsimd", lambda e: e.indirect_dma_start(
                answers, bass.IndirectOffsetOnAxis(ap=dest[j % ND][:, 0:1], axis=0), z[j % NZ][:, :], None),
                [done["z", j], done["dest", j]], s_ans[j % NZ], 16)

        done["phase"] = done["gate"]

        T = 2.4
        for j in range(SLOT_TILES):
            for time, step in ((0.5 - NX * T, b_load), (-0.2, b_dest), (0.0, b_turn), (0.05, b_turn_copy),
                               (0.36, b_up), (1.13, b_relu), (2.73, b_turn_r), (2.93, b_rT_hi),
                               (3.09, b_stats), (3.55, b_aggr), (4.76, b_std), (5.15, b_rT_lo),
                               (6.05, b_rstd), (7.24, b_down), (7.56, b_affine), (7.62, b_relu2),
                               (8.22, b_stats2), (8.56, b_aggr2), (9.72, b_std2), (10.0, b_rstd2),
                               (10.31, b_norm), (10.4, b_out), (10.94, b_answer)):
                at(j * T + time, step, j)
            for name, time in (("tensor", 0.1), ("vector", 5.5), ("gpsimd", 8.6)):
                if j % PACK == 0:
                    at(j * T + time - T * (j > 0), b_pack, j // PACK, name)
        queue_plan()

        s_ya = [signal(f"back{g}") for g in range(GROUPS)]
        s_c = signal("combined")
        s_out = signal("stored")
        answered = [done["answer", SLOT_TILES - 1 - n] for n in range(NZ)]
        for g in range(GROUPS):
            tiles = slice(g * GT, (g + 1) * GT)
            for k in range(K):
                t = pr.add("sync", lambda e, k=k, g=g: e.dma_start(
                    ya[g][:, k, :, :], ans_v[:, k * TILES + g * GT:k * TILES + (g + 1) * GT, :]),
                    answered, s_ya[g], 16)
            loaded, first = t, {}
            for k in range(K):
                for i in range(GT):
                    n = g * GT + i
                    t = pr.add("vector", lambda e, g=g, i=i, n=n, k=k: e.scalar_tensor_tensor(
                        out=res[g][:, i, :], in0=ya[g][:, k, i, :], scalar=gate[:, k, n:n + 1],
                        in1=res[g][:, i, :] if k else x2[:, n, :], op0=ALU.mult, op1=ALU.add),
                        [first[i] if k else loaded], s_c)
                    first[i] = t
            stored = pr.add("scalar", lambda e, g=g, tiles=tiles: e.dma_start(
                out_v[:, tiles, :], res[g][:, :, :]), [t], s_out, 16)

        final = [stored, done["zeroed"], *scattered, *answered]

        block = ctx.enter_context(nc.Block())
        for name in ("sync", "gpsimd", "scalar", "tensor", "vector"):
            def body(eng, name=name):
                for run in pr.queues[name]:
                    run(eng)
                if name == "sync":
                    for sig, value in final:
                        eng.wait_ge(sig.handle, value)
            {"sync": block.sync, "gpsimd": block.gpsimd, "scalar": block.scalar, "tensor": block.tensor,
             "vector": block.vector}[name](body)


_INS = ["x", "ctx_1024", "L0_xattn_Wk", "L0_xattn_Wv", "L0_xattn_bv", "L0_xattn_Wq", "L0_xattn_bq",
        "L0_xattn_Wo", "L0_xattn_bo", "L0_ffn_Wr", "L0_ffn_br", "L0_ffn_W1", "L0_ffn_b1", "L0_ffn_g1",
        "L0_ffn_be1", "L0_ffn_W2", "L0_ffn_b2", "L0_ffn_g2", "L0_ffn_be2"]


def kernel(**inputs):
    import concourse.bacc as bacc
    from concourse.bass_utils import run_bass_kernel_spmd

    nc = bacc.Bacc("TRN2", target_bir_lowering=False, num_devices=1)
    arrays, args = {}, {}
    for name in _INS:
        a = np.ascontiguousarray(inputs[name])
        arrays[f"in_{name}"] = a
        args[name] = nc.dram_tensor(f"in_{name}", a.shape, mybir.dt.from_np(a.dtype),
                                    kind="ExternalInput").ap()
    out = nc.dram_tensor("out_0", inputs["x"].shape, mybir.dt.float32, kind="ExternalOutput").ap()
    build(nc, args, out)
    r = run_bass_kernel_spmd(nc, [arrays], core_ids=[0])
    return r.results[0]["out_0"]
```
